# Optimizing a Trainium2 kernel written in Bass

```python
import numpy as np
import jax
import jax.numpy as jnp

def _softmax(x, axis=-1):
    return jax.nn.softmax(x, axis=axis)

def _gelu(x):
    return jax.nn.gelu(x, approximate=True)

def _silu(x):
    return jax.nn.silu(x)

def _sigmoid(x):
    return jax.nn.sigmoid(x)

def _layernorm(x, axis=-1, eps=1e-05):
    m = jnp.mean(x, axis=axis, keepdims=True)
    v = jnp.var(x, axis=axis, keepdims=True)
    return (x - m) / jnp.sqrt(v + eps)

def _scatter_add(tgt, idx, src, axis=0):
    return tgt.at[idx].add(src)

def _segment_sum(src, seg, n):
    return jax.ops.segment_sum(src, seg, n)
kernel_name = 'mk_sandwich_d1_jaxref_r4_3dfba7'

def setup_inputs(seed: int=0):
    np.random.seed(seed)
    _w = jnp.asarray

    def _L0_attn_setup():
        import jax, jax.numpy as jnp
        import numpy as np
        import math
        EMBED_DIM = 512
        NUM_HEADS = 16
        HEAD_DIM = EMBED_DIM // NUM_HEADS
        SCALE = 1.0 / math.sqrt(HEAD_DIM)
        _BASE = 2.0 ** (-2.0 ** (-(math.log2(NUM_HEADS) - 3)))
        ALIBI_SLOPES = np.array([_BASE ** i for i in range(1, NUM_HEADS + 1)], dtype=np.float32)
        key = jax.random.key(seed)
        ks = jax.random.split(key, 7)
        B, L, D, R_KV, R_Q = (2, 512, EMBED_DIM, 128, 384)
        std = 0.02
        return {'hidden_states': jax.random.normal(ks[0], (B, L, D), jnp.float32), 'Wq_down': jax.random.normal(ks[1], (R_Q, D), jnp.float32) * std, 'Wq_up': jax.random.normal(ks[2], (NUM_HEADS * HEAD_DIM, R_Q), jnp.float32) * std, 'Wkv_down': jax.random.normal(ks[3], (R_KV, D), jnp.float32) * std, 'k_up': jax.random.normal(ks[4], (NUM_HEADS, R_KV, HEAD_DIM), jnp.float32) * std, 'v_up': jax.random.normal(ks[5], (NUM_HEADS, R_KV, HEAD_DIM), jnp.float32) * std, 'Wo': jax.random.normal(ks[6], (D, D), jnp.float32) * std}
    _L0_attn_in = _L0_attn_setup()

    def _L0_ffn_setup():
        import jax, jax.numpy as jnp
        import numpy as np
        _FP4_LUT = jnp.array([0.0, 0.5, 1.0, 1.5, 2.0, 3.0, 4.0, 6.0, -0.0, -0.5, -1.0, -1.5, -2.0, -3.0, -4.0, -6.0], dtype=jnp.float32)
        GROUP_SIZE = 128
        EPS = 1e-06

        def _dequant_fp4(packed_i32, scales_f16, group_size):
            out_f, in_p = packed_i32.shape
            w = packed_i32.astype(jnp.uint32)
            shifts = jnp.arange(8, dtype=jnp.uint32) * 4
            nib = w[:, :, None] >> shifts & jnp.uint32(15)
            vals = _FP4_LUT[nib.astype(jnp.int32)].reshape(out_f, in_p * 8)
            s = scales_f16.astype(jnp.float32).T
            s_full = jnp.repeat(s, group_size, axis=1)
            return vals * s_full
        key = jax.random.key(seed)
        k1, k2, k3, k4, k5 = jax.random.split(key, 5)
        B, S, H, I = (4, 512, 512, 1408)
        x = jax.random.normal(k1, (B, S, H), dtype=jnp.float32)
        gate_up_packed = jax.random.randint(k2, (2 * I, H // 8), 0, 2147483647, dtype=jnp.int32)
        gate_up_scales = jax.random.uniform(k3, (H // GROUP_SIZE, 2 * I), dtype=jnp.float32).astype(jnp.float16)
        down_packed = jax.random.randint(k4, (H, I // 8), 0, 2147483647, dtype=jnp.int32)
        down_scales = jax.random.uniform(k5, (I // GROUP_SIZE, H), dtype=jnp.float32).astype(jnp.float16)
        return {'x': x, 'gate_up_packed': gate_up_packed, 'gate_up_scales': gate_up_scales, 'down_packed': down_packed, 'down_scales': down_scales}
    _L0_ffn_in = _L0_ffn_setup()
    _d = {'L0_attn_hidden_states': _L0_attn_in['hidden_states'], 'L0_attn_Wq_down': _L0_attn_in['Wq_down'], 'L0_attn_Wq_up': _L0_attn_in['Wq_up'], 'L0_attn_Wkv_down': _L0_attn_in['Wkv_down'], 'L0_attn_k_up': _L0_attn_in['k_up'], 'L0_attn_v_up': _L0_attn_in['v_up'], 'L0_attn_Wo': _L0_attn_in['Wo'], 'L0_ffn_gate_up_packed': _L0_ffn_in['gate_up_packed'], 'L0_ffn_gate_up_scales': _L0_ffn_in['gate_up_scales'], 'L0_ffn_down_packed': _L0_ffn_in['down_packed'], 'L0_ffn_down_scales': _L0_ffn_in['down_scales']}
    _x0 = _d['L0_attn_hidden_states']
    _d['L0_attn_hidden_states'] = jax.random.normal(jax.random.fold_in(jax.random.key(seed), 1), (16, 512, 512), dtype=_x0.dtype)
    del _x0
    return _d

def reference(L0_attn_hidden_states, L0_attn_Wq_down, L0_attn_Wq_up, L0_attn_Wkv_down, L0_attn_k_up, L0_attn_v_up, L0_attn_Wo, L0_ffn_gate_up_packed, L0_ffn_gate_up_scales, L0_ffn_down_packed, L0_ffn_down_scales):

    def _L0_attn_ref(hidden_states, Wq_down, Wq_up, Wkv_down, k_up, v_up, Wo):
        import jax, jax.numpy as jnp
        import numpy as np
        import math
        EMBED_DIM = 512
        NUM_HEADS = 16
        HEAD_DIM = EMBED_DIM // NUM_HEADS
        SCALE = 1.0 / math.sqrt(HEAD_DIM)
        _BASE = 2.0 ** (-2.0 ** (-(math.log2(NUM_HEADS) - 3)))
        ALIBI_SLOPES = np.array([_BASE ** i for i in range(1, NUM_HEADS + 1)], dtype=np.float32)
        B, L, D = hidden_states.shape
        q = hidden_states @ Wq_down.T @ Wq_up.T
        q = q.reshape(B, L, NUM_HEADS, HEAD_DIM).transpose(0, 2, 1, 3)
        c = hidden_states @ Wkv_down.T
        k = jnp.einsum('bsr,hrd->bhsd', c, k_up)
        v = jnp.einsum('bsr,hrd->bhsd', c, v_up)
        scores = jnp.einsum('bhqd,bhkd->bhqk', q, k) * SCALE
        pos = jnp.arange(L)
        dist = jnp.abs(pos[:, None] - pos[None, :]).astype(jnp.float32)
        slopes = jnp.asarray(ALIBI_SLOPES)
        scores = scores - slopes[None, :, None, None] * dist[None, None, :, :]
        causal = pos[:, None] >= pos[None, :]
        scores = jnp.where(causal[None, None], scores, -jnp.inf)
        attn = jax.nn.softmax(scores.astype(jnp.float32), axis=-1).astype(scores.dtype)
        out = jnp.einsum('bhqk,bhkd->bhqd', attn, v)
        out = out.transpose(0, 2, 1, 3).reshape(B, L, D)
        return out @ Wo.T

    def _L0_ffn_ref(x, gate_up_packed, gate_up_scales, down_packed, down_scales):
        import jax, jax.numpy as jnp
        import numpy as np
        _FP4_LUT = jnp.array([0.0, 0.5, 1.0, 1.5, 2.0, 3.0, 4.0, 6.0, -0.0, -0.5, -1.0, -1.5, -2.0, -3.0, -4.0, -6.0], dtype=jnp.float32)
        GROUP_SIZE = 128
        EPS = 1e-06

        def _dequant_fp4(packed_i32, scales_f16, group_size):
            out_f, in_p = packed_i32.shape
            w = packed_i32.astype(jnp.uint32)
            shifts = jnp.arange(8, dtype=jnp.uint32) * 4
            nib = w[:, :, None] >> shifts & jnp.uint32(15)
            vals = _FP4_LUT[nib.astype(jnp.int32)].reshape(out_f, in_p * 8)
            s = scales_f16.astype(jnp.float32).T
            s_full = jnp.repeat(s, group_size, axis=1)
            return vals * s_full
        I = gate_up_packed.shape[0] // 2
        w_gu = _dequant_fp4(gate_up_packed, gate_up_scales, GROUP_SIZE)
        w_down = _dequant_fp4(down_packed, down_scales, GROUP_SIZE)
        gate_up = jnp.einsum('bsh,oh->bso', x, w_gu)
        gate, up = (gate_up[..., :I], gate_up[..., I:])
        h = jax.nn.silu(gate) * up
        y = jnp.einsum('bsi,hi->bsh', h, w_down)
        rms = jnp.sqrt(jnp.mean(y * y, axis=-1, keepdims=True) + EPS)
        return y / rms
    x = L0_attn_hidden_states
    x = x + _layernorm(_L0_attn_ref(_layernorm(x, axis=-1), L0_attn_Wq_down, L0_attn_Wq_up, L0_attn_Wkv_down, L0_attn_k_up, L0_attn_v_up, L0_attn_Wo), axis=-1)
    x = x + _layernorm(_L0_ffn_ref(_layernorm(x, axis=-1), L0_ffn_gate_up_packed, L0_ffn_gate_up_scales, L0_ffn_down_packed, L0_ffn_down_scales), axis=-1)
    return x

_drawn_inputs = setup_inputs


def setup_inputs(seed=0):
    import zlib

    import numpy as np

    out = dict(_drawn_inputs(seed))
    spreads = {}
    factors = {'L0_attn_Wq_down': 4.225, 'L0_attn_Wq_up': 4.171, 'L0_attn_k_up': 4.197}
    for name, (base, spread) in spreads.items():
        noise = np.random.default_rng([zlib.crc32(name.encode()), seed]).standard_normal(out[name].shape)
        drawn = base * np.exp(spread * noise) if base else spread * noise
        out[name] = jnp.asarray(drawn.astype(out[name].dtype))
    for name, factor in factors.items():
        out[name] = (out[name] * factor).astype(out[name].dtype)
    return out
```

```python
from contextlib import ExitStack

import concourse.bass as bass
import numpy as np
from concourse import mybir

B, L, D = 16, 512, 512
H, HD = 16, 32
RQ, RKV = 384, 128
I = 1408
P = 128
NT = L // P
KC = D // P
HG = P // HD
NG = H // HG
MI = I // P
GROUPS = D // P
UNITS = 2 * MI + MI

S_X, S_W, S_WQ, S_W4 = 2.0 ** 4, 2.0 ** 8, 2.0 ** 6, 2.0 ** 6
S_C, S_QK, S_V, S_H = 2.0 ** 4, 2.0 ** 4, 2.0 ** 6, 2.0 ** -8
S_SCORE = S_QK * S_QK
ROW_MAX = 1024.0
FP8_SCALE = 2.0 ** 6
EPS, RMS_EPS = 1e-5, 1e-6

COUNTS = {
    "dense": (0, 18, 52, 52), "free": (0, 18, 52, 52), "hi": (0, 13, 17, 17),
    "mx": (0, 64, 64, 64), "mxfree": (0, 64, 64, 64), "mh": (0, 1, 1, 1), "mrow": (0, 16, 16, 16),
    "st": (0, 64, 64, 64), "exp": (0, 64, 64, 64), "pv": (0, 4, 4, 4), "on": (0, 4, 4, 4),
    "oh": (0, 4, 4, 4), "ol": (0, 4, 4, 4), "stk": (0, 384, 384, 384), "xin": (16, 16, 16, 0),
    "xres": (64, 0, 64, 64), "ln1": (4, 4, 4, 0), "ve": (1, 1, 7, 6), "rs": (1, 1, 7, 6),
    "z2": (0, 0, 4, 4), "add2": (0, 0, 4, 4), "ln3": (0, 0, 4, 4), 
    "po": (0, 0, 4, 4), "out0": (16, 0, 32, 32), "out1": (16, 0, 32, 32), "tanh": (0, 0, 11, 11), "hh": (0, 0, 11, 11),
    "hl": (0, 0, 11, 11), "chain": (8, 12, 44, 36),
}
ATT_JOBS = {"P1": 0, "C": 4, "Q": 5, "K": 9, "V": 13, "MT": 17}
BOTH_JOBS = {"P1": 0, "WO": 4, "C": 8, "Q": 9, "K": 13, "V": 17, "X2": 21, "F": 25, "MT": 35, "G": 36, "D": 48}
FFN_JOBS = {"WO": 0, "X2": 4, "F": 8, "D": 30}
F_EARLY = 5


def layer_program(nc, x, wq_down, wq_up_t, wkv_down_t, k_up_t, v_up_t, wo_t, gu_packed, gu_scales,
                  dn_packed, dn_scales, aug_q, aug_k, tri, eye32, eye16, eye_big, out):
    f32, f16, bf16 = mybir.dt.float32, mybir.dt.float16, mybir.dt.bfloat16
    i32, fp8 = mybir.dt.int32, mybir.dt.float8e4
    ACT, ALU = mybir.ActivationFunctionType, mybir.AluOpType

    ctx = ExitStack()
    with ctx:
        def sb(name, shape, dt):
            return ctx.enter_context(nc.sbuf_tensor(name, shape, dt))

        wq = sb("wq", [P, 2, KC, D], f16)
        wkv = sb("wkv", [P, 2, KC, RKV], f16)
        kup = sb("kup", [P, 2, D], f16)
        vup = sb("vup", [P, 2, D], f16)
        wo = sb("wo", [P, 2, KC, D], f16)
        wgu = sb("wgu", [P, 2, KC, 2 * I], f16)
        wdn = sb("wdn", [P, 2, MI, D], f16)
        xin = sb("xin", [P, NT, D], f32)
        x1 = sb("x1", [P, NT, D], f32)
        stage = sb("stage", [P, 2, D], f32)
        tb = sb("tb", [P, 2, L], f32)
        rec = sb("rec", [P, L], f32)
        ct = sb("ct", [P, 2, L], f16)
        qst = sb("qst", [P, H, L], f16)
        kst = sb("kst", [P, H, L], f16)
        HT0 = NT * D
        P0 = HT0 + 2 * MI * L // 2
        O0 = P0 + HG * L
        X20 = O0 + 2 * KC * L // 2
        arena = sb("arena", [P, X20 + 2 * KC * L // 2], f32)
        v = arena[:, 0:HT0].rearrange("p (a b) -> p a b", a=NT)
        z = v
        ht = arena[:, HT0:P0].bitcast(f16).rearrange("p (s a b) -> p s a b", s=2, a=MI)
        qk = arena[:, HT0:HT0 + 4 * NG * L // 2].bitcast(f16).rearrange("p (s a b) -> p s a b", s=4, a=NG)
        prob = arena[:, P0:O0].rearrange("p (a b) -> p a b", a=HG)
        xt = arena[:, P0:O0].bitcast(f16).rearrange("p (s a b) -> p s a b", s=2, a=KC)
        ot = arena[:, O0:X20].bitcast(f16).rearrange("p (s a b) -> p s a b", s=2, a=NG)
        xn2 = arena[:, O0:X20].rearrange("p (a b) -> p a b", a=NT)
        x2t = arena[:, X20:X20 + KC * L].bitcast(f16).rearrange("p (s a b) -> p s a b", s=2, a=KC)
        GUW, DNW = 2 * MI * (D // 8), KC * (I // 8)
        W = GUW + DNW
        packed = arena[:, 0:W].bitcast(i32)
        bits1 = arena[:, W:2 * W].bitcast(i32)
        bits2 = arena[:, 2 * W:3 * W].bitcast(i32)
        codes = arena[:, 3 * W:5 * W].bitcast(i32).rearrange("p (e w) -> p e w", e=2)
        codes8 = arena[:, 3 * W:5 * W].bitcast(fp8).rearrange("p (e w) -> p e w", e=2)
        wblk = arena[:, 5 * W:5 * W + 4 * D].rearrange("p (r a b) -> p r a b", r=4, a=4)
        qf = qst[:, :, :].rearrange("p a b -> p (a b)").bitcast(f32)
        kf = kst[:, :, :].rearrange("p a b -> p (a b)").bitcast(f32)
        raw_wqd = qf[:, 0:3 * D].rearrange("p (a b) -> p a b", a=3)
        raw_wqu = qf[:, 3 * D:6 * D].rearrange("p (a b) -> p a b", a=3)
        raw_kup = qf[:, 6 * D:7 * D]
        raw_vup = qf[:, 7 * D:8 * D]
        raw_wkv = kf[:, 0:D].rearrange("p (a b) -> p a b", a=KC)
        raw_wo = kf[:, D:5 * D].rearrange("p (a b) -> p a b", a=KC)
        sc16 = sb("sc16", [P, 2 * MI * GROUPS + KC * MI], f16)
        sc32 = sb("sc32", [P, 2 * MI * GROUPS + KC * MI], f32)
        mmax = sb("mmax", [P, L], bf16)
        tri_sb = sb("tri_sb", [P, P], f16)
        id32 = sb("id32", [P, P], f32)
        id16 = sb("id16", [P, P], f16)
        idbig = sb("idbig", [P, P], f16)
        ones = sb("ones", [P, HD], f32)
        mcol = sb("mcol", [P, H * NT], f32)
        mh = sb("mh", [P, H * NT], f16)
        mrow = sb("mrow", [H * NT, P], f16)
        half = sb("half", [P, NT], f32)
        st6 = {n: sb("st6_" + n, [P, NT, 6], f32) for n in ("ln1", "ln2", "ln3", "lo")}
        mv = {n: sb("mv_" + n, [P, NT, 2], f32) for n in ("ln1", "ln2", "ln3", "lo")}
        ve = {n: sb("ve_" + n, [P, NT], f32) for n in ("ln1", "ln2", "ln3", "lo")}
        rs = {n: sb("rs_" + n, [P, NT], f32) for n in ("ln1", "ln2", "ln3", "lo")}

        def ps(name):
            return ctx.enter_context(nc.psum_tensor(name, [P, 512], f32))
        dense = [ps(f"dense{i}") for i in range(4)]
        score = [ps(f"score{i}") for i in range(2)]
        psO, psSum = ps("psO"), ps("psSum")

        sem = {n: ctx.enter_context(nc.semaphore("s_" + n)) for n in COUNTS}
        s_w = ctx.enter_context(nc.semaphore("s_w"))
        s_w4 = ctx.enter_context(nc.semaphore("s_w4"))
        s_const = ctx.enter_context(nc.semaphore("s_const"))
        s_aug = ctx.enter_context(nc.semaphore("s_aug"))
        s_passed_v = ctx.enter_context(nc.semaphore("s_passed_v"))
        s_passed_t = ctx.enter_context(nc.semaphore("s_passed_t"))
        s_mask = ctx.enter_context(nc.semaphore("s_mask"))
        s_ones = ctx.enter_context(nc.semaphore("s_ones"))
        s_half = ctx.enter_context(nc.semaphore("s_half"))
        s_bits = ctx.enter_context(nc.semaphore("s_bits"))
        s_prep_mm = ctx.enter_context(nc.semaphore("s_prep_mm"))
        s_prep_hi = ctx.enter_context(nc.semaphore("s_prep_hi"))
        s_prep_lo = ctx.enter_context(nc.semaphore("s_prep_lo"))
        s_raw_hi = ctx.enter_context(nc.semaphore("s_raw_hi"))
        s_raw_lo = ctx.enter_context(nc.semaphore("s_raw_lo"))
        s_blk_a = ctx.enter_context(nc.semaphore("s_blk_a"))
        s_blk_v = ctx.enter_context(nc.semaphore("s_blk_v"))

        def val(name, t, k):
            pre, n0, nb, n_last = COUNTS[name]
            if isinstance(t, int) and t == 0:
                return pre + k
            if isinstance(t, int) and t == B:
                return pre + n0 + nb * (B - 2) + n_last + k
            return nb * t + (pre + n0 - nb + k)

        def jobs(t):
            if isinstance(t, int) and t == 0:
                return ATT_JOBS
            return FFN_JOBS if isinstance(t, int) and t == B else BOTH_JOBS

        def job_f(t, m, up):
            j = jobs(t)
            if "G" in j and m >= F_EARLY:
                return j["G"] + 2 * (m - F_EARLY) + up
            return j["F"] + 2 * m + up

        def bank(t, n):
            pre, n0, nb, n_last = COUNTS["dense"]
            start = 0 if isinstance(t, int) and t == 0 else n0
            return (start + n) % 4

        def terms(w, a, n):
            out_ = []
            for c in range(n):
                out_ += [(w(0, c), a(0, c)), (w(0, c), a(1, c)), (w(1, c), a(0, c))]
            return out_

        def block_of(u, g):
            if u < 2 * MI:
                w0, k = (D // 8) * u + 16 * g, GROUPS * u + g
            else:
                m = u - 2 * MI
                w0, k = GUW + (I // 8) * g + 16 * m, 2 * MI * GROUPS + MI * g + m
            return codes8[:, :, 4 * w0:4 * w0 + 64], k

        def unit_dst(u, s):
            if u < 2 * MI:
                return wgu[:, s, :, P * u:P * u + P]
            return wdn[:, s, u - 2 * MI, :].rearrange("p (a b) -> p a b", a=4)

        block = ctx.enter_context(nc.Block())

        @block.tensor
        def _(pe):
            def open_job(t, n):
                if isinstance(t, int) and t == 0 and n < 4:
                    return
                pe.wait_ge(sem["free"], val("free", t, n - 3))

            def products(dst, tt, first=True, last=True):
                for k, (w, a) in enumerate(tt):
                    ins = nc.tensor.matmul(dst, w, a, start=first and k == 0, stop=last and k == len(tt) - 1)
                return ins

            def transposes(t, n, src):
                for i in range(NT):
                    ins = nc.tensor.transpose(dense[bank(t, n)][:, P * i:P * i + P], src(i), id32[:, :])
                ins.then_inc(sem["dense"], 1)

            def prepare():
                pe.wait_ge(s_const, 64)
                pe.wait_ge(s_ones, 1)
                pe.wait_ge(s_w, 96)
                for c in range(KC):
                    for r in range(3):
                        ins = nc.tensor.matmul(dense[c][:, :], raw_wqd[:, r, P * c:P * c + P], raw_wqu[:, r, :],
                                               start=r == 0, stop=r == 2)
                    ins.then_inc(s_prep_mm, 1)
                for u in range(UNITS):
                    pe.wait_ge(s_prep_lo, u + 1)
                    pe.wait_ge(s_blk_v if u % 2 else s_blk_a, 4 * (u // 2) + 4)
                    for g in range(4):
                        ins = nc.tensor.transpose(dense[u % 4][:, P * g:P * g + P], wblk[:, u % 4, g, :], id32[:, :])
                    ins.then_inc(s_prep_mm, 1)
                pe.wait_ge(s_prep_lo, KC + UNITS)
                pe.wait_ge(s_raw_lo, 4)

            def step(t, att, ffn, nxt):
                j = jobs(t)
                if att:
                    pe.wait_ge(sem["ln1"], val("ln1", t, 0) if not (isinstance(t, int) and t == 0) else 4)
                    for c in range(KC):
                        open_job(t, j["P1"] + c)
                        transposes(t, j["P1"] + c, lambda i: xin[:, i, P * c:P * c + P])
                if ffn:
                    pe.wait_ge(sem["ol"], val("ol", t, 0))
                    for i in range(NT):
                        open_job(t, j["WO"] + i)
                        products(dense[bank(t, j["WO"] + i)][:, :],
                                 terms(lambda s, c: ot[:, s, c, P * i:P * i + P], lambda s, c: wo[:, s, c, :], KC)
                                 ).then_inc(sem["dense"], 1)
                if att:
                    pe.wait_ge(sem["free"], val("free", t, j["P1"] + 4))
                    open_job(t, j["C"])
                    products(dense[bank(t, j["C"])][:, :],
                             terms(lambda s, c: wkv[:, s, c, :], lambda s, c: xt[:, s, c, :], KC)
                             ).then_inc(sem["dense"], 1)
                    for g in range(NG):
                        open_job(t, j["Q"] + g)
                        products(dense[bank(t, j["Q"] + g)][:, :],
                                 terms(lambda s, c: wq[:, s, c, P * g:P * g + P], lambda s, c: xt[:, s, c, :], KC)
                                 ).then_inc(sem["dense"], 1)
                    pe.wait_ge(sem["free"], val("free", t, j["C"] + 1))
                    for g in range(NG):
                        open_job(t, j["K"] + g)
                        products(dense[bank(t, j["K"] + g)][:, :],
                                 terms(lambda s, c: kup[:, s, P * g:P * g + P], lambda s, c: ct[:, s, :], 1)
                                 ).then_inc(sem["dense"], 1)
                    for i in range(NT):
                        open_job(t, j["V"] + i)
                        products(dense[bank(t, j["V"] + i)][:, :],
                                 terms(lambda s, c: ct[:, s, P * i:P * i + P], lambda s, c: vup[:, s, :], 1)
                                 ).then_inc(sem["dense"], 1)
                if ffn:
                    pe.wait_ge(sem["ln3"], val("ln3", t, 4))
                    for c in range(KC):
                        open_job(t, j["X2"] + c)
                        transposes(t, j["X2"] + c, lambda i: xn2[:, i, P * c:P * c + P])
                    pe.wait_ge(sem["free"], val("free", t, j["X2"] + 4))

                def ffn_up(m, up, a, b):
                    n = job_f(t, m, up)
                    if a == 0:
                        open_job(t, n)
                    col = I * up + P * m
                    tt = terms(lambda s, c: wgu[:, s, c, col:col + P], lambda s, c: x2t[:, s, c, :], KC)
                    ins = products(dense[bank(t, n)][:, :], tt[a:b], a == 0, b == 12)
                    if b == 12:
                        ins.then_inc(sem["dense"], 1)

                def ffn_down(i, part):
                    n = j["D"] + i
                    if part == 0:
                        open_job(t, n)
                    tt = terms(lambda s, m: ht[:, s, m, P * i:P * i + P], lambda s, m: wdn[:, s, m, :], MI)
                    pe.wait_ge(sem["hl"], val("hl", t, 6 if part == 0 else MI))
                    ins = products(dense[bank(t, n)][:, :], tt[:18] if part == 0 else tt[18:], part == 0, part == 1)
                    if part == 1:
                        ins.then_inc(sem["dense"], 1)

                if not att:
                    for m in range(MI):
                        ffn_up(m, 0, 0, 12)
                        ffn_up(m, 1, 0, 12)
                    for i in range(NT):
                        ffn_down(i, 0)
                        ffn_down(i, 1)
                    return
                if isinstance(t, int) and t == 0:
                    pe.wait_ge(s_aug, 32)
                pe.wait_ge(sem["stk"], val("stk", t, 384))
                for h in range(H):
                    for i in range(NT):
                        k = NT * h + i
                        if k >= 2:
                            pe.wait_ge(sem["mxfree"], val("mxfree", t, k - 1))
                        nc.tensor.matmul(score[k % 2][:, 0:P * (i + 1)], qst[0:P - 1, h, P * i:P * i + P],
                                         kst[0:P - 1, h, 0:P * (i + 1)], start=True, stop=True).then_inc(sem["mx"], 1)
                        slot = 2 * h + i // 2
                        if ffn and i % 2 == 1 and slot < 6 * F_EARLY:
                            part = slot % 3
                            ffn_up(slot // 6, slot % 6 // 3, 4 * part, 4 * part + 4)
                pe.wait_ge(sem["mh"], val("mh", t, 1))
                open_job(t, j["MT"])
                pe.sem_inc(s_passed_t, 1)
                nc.tensor.transpose(dense[bank(t, j["MT"])][0:H * NT, 0:P // 2].bitcast(f16), mh[:, :],
                                    id16[:, :]).then_inc(sem["dense"], 1)
                if ffn:
                    ffn_up(F_EARLY, 0, 0, 12)
                    ffn_up(F_EARLY, 1, 0, 12)
                pe.wait_ge(sem["mrow"], val("mrow", t, 16))

                def filler(s, part):
                    if not ffn:
                        return
                    if s < 10:
                        ffn_up(F_EARLY + 1 + s // 2, s % 2, 6 * part, 6 * part + 6)
                    elif part == 0:
                        ffn_down((s - 10) // 2, (s - 10) % 2)

                for s in range(NG * NT):
                    g, kt = s // NT, s % NT
                    wide = L - P * kt
                    for a in range(HG):
                        h, e = HG * g + a, HG * s + a
                        if e >= 2:
                            pe.wait_ge(sem["exp"], val("exp", t, e - 1))
                        nc.tensor.matmul(score[e % 2][:, 0:wide], kst[:, h, P * kt:P * kt + P],
                                         qst[:, h, P * kt:L], start=True, stop=False)
                        nc.tensor.matmul(score[e % 2][:, 0:P], idbig[:, :], tri_sb[:, :],
                                         start=False, stop=True).then_inc(sem["st"], 1)
                        if a % 2 == 1:
                            filler(s, a // 2)
                    pe.wait_ge(sem["exp"], val("exp", t, HG * s + HG))
                    if kt == 0 and g > 0:
                        pe.wait_ge(sem["on"], val("on", t, g))
                    for a in range(HG):
                        nc.tensor.matmul(psO[HD * a:HD * a + HD, P * kt:L], v[:, kt, HD * (HG * g + a):HD * (HG * g + a) + HD],
                                         prob[:, a, 0:wide], start=kt == 0, stop=kt == NT - 1)
                    for a in range(HG):
                        ins = nc.tensor.matmul(psSum[HD * a:HD * a + HD, P * kt:L], ones[:, :],
                                               prob[:, a, 0:wide], start=kt == 0, stop=kt == NT - 1)
                    if kt == NT - 1:
                        ins.then_inc(sem["pv"], 1)
                if ffn:
                    ffn_down(NT - 1, 0)
                    ffn_down(NT - 1, 1)

            prepare()
            step(0, True, False, True)
            with pe.Fori(1, B - 1) as t:
                step(t, True, True, True)
            step(B - 1, True, True, False)
            step(B, False, True, False)

        @block.scalar
        def _(act):
            def prepare():
                act.wait_ge(s_w, 96)
                for n, (dst, src) in enumerate(((kup[:, 0, :], raw_kup), (vup[:, 0, :], raw_vup),
                                                (wkv[:, 0, :, :], raw_wkv), (wo[:, 0, :, :], raw_wo))):
                    nc.scalar.activation(dst, src, ACT.Copy, scale=S_W).then_inc(s_raw_hi, 1)

                def dequantise(u):
                    act.wait_ge(s_bits, 7)
                    if u >= 4:
                        act.wait_ge(s_prep_mm, KC + u - 3)
                    for g in range(4):
                        src, k = block_of(u, g)
                        nc.scalar.activation(wblk[:, u % 4, g, :].rearrange("p (j e) -> p e j", e=2), src, ACT.Copy,
                                             scale=sc32[:, k:k + 1]).then_inc(s_blk_a, 1)

                def high(n, dst, src, scale):
                    act.wait_ge(s_prep_mm, n + 1)
                    nc.scalar.activation(dst, src, ACT.Copy, scale=scale).then_inc(s_prep_hi, 1)

                for c in range(KC):
                    high(c, wq[:, 0, c, :], dense[c][:, :], S_WQ)
                dequantise(0)
                for u in range(UNITS):
                    if u % 2 == 1 and u + 1 < UNITS:
                        dequantise(u + 1)
                    high(KC + u, unit_dst(u, 0), dense[u % 4][:, :].rearrange("p (a b) -> p a b", a=4), 1.0)

            def step(t, att, ffn, nxt):
                j = jobs(t)
                hi = [0]

                def high(n, dst, scale):
                    act.wait_ge(sem["dense"], val("dense", t, n + 1))
                    nc.scalar.activation(dst, dense[bank(t, n)][:, :], ACT.Copy, scale=scale).then_inc(sem["hi"], 1)

                def tanh(m):
                    if m >= 2:
                        act.wait_ge(sem["hl"], val("hl", t, m - 1))
                    n = job_f(t, m, 0)
                    act.wait_ge(sem["dense"], val("dense", t, n + 1))
                    nc.scalar.activation(tb[:, m % 2, :], dense[bank(t, n)][:, :], ACT.Tanh,
                                         scale=0.5 / (S_X * S_W4)).then_inc(sem["tanh"], 1)

                def h_high(m):
                    act.wait_ge(sem["free"], val("free", t, job_f(t, m, 1) + 1))
                    nc.scalar.activation(ht[:, 0, m, :], tb[:, m % 2, :], ACT.Copy,
                                         scale=S_H / (2 * (S_X * S_W4) ** 2)).then_inc(sem["hh"], 1)

                def o_high(g):
                    act.wait_ge(sem["on"], val("on", t, g + 1))
                    nc.scalar.activation(ot[:, 0, g, :], rec[:, :], ACT.Copy).then_inc(sem["oh"], 1)

                if att:
                    for c in range(KC):
                        high(j["P1"] + c, xt[:, 0, c, :], S_X)
                    high(j["C"], ct[:, 0, :], S_C / (S_X * S_W))
                    for g in range(NG):
                        high(j["Q"] + g, qk[:, 0, g, :], HD ** -0.5 * S_QK / (S_X * S_WQ))
                    for g in range(NG):
                        high(j["K"] + g, qk[:, 2, g, :], S_QK / (S_C * S_W))
                if ffn:
                    for c in range(KC):
                        high(j["X2"] + c, x2t[:, 0, c, :], S_X)
                if not att:
                    for m in range(MI):
                        tanh(m)
                        h_high(m)
                    return
                if ffn:
                    for m in range(F_EARLY + 1):
                        tanh(m)
                        h_high(m)
                for s in range(NG * NT):
                    wide = L - P * (s % NT)
                    for a in range(HG):
                        e = HG * s + a
                        act.wait_ge(sem["st"], val("st", t, e + 1))
                        nc.scalar.activation(prob[:, a, 0:wide], score[e % 2][:, 0:wide], ACT.Exp,
                                             scale=1.0 / S_SCORE).then_inc(sem["exp"], 1)
                    if ffn and s % 2 == 0 and s < 10:
                        tanh(F_EARLY + 1 + s // 2)
                    if ffn and s % 2 == 0 and 2 <= s <= 10:
                        h_high(F_EARLY + s // 2)
                    if s % NT == 0 and s > 0:
                        o_high(s // NT - 1)
                o_high(NG - 1)

            prepare()
            step(0, True, False, True)
            with act.Fori(1, B - 1) as t:
                step(t, True, True, True)
            step(B - 1, True, True, False)
            step(B, False, True, False)

        @block.vector
        def _(dve):
            chain = [0]

            def link(t, ins):
                chain[0] += 1
                ins.then_inc(sem["chain"], 1)

            def apart():
                dve.sem_inc(s_passed_v, 1)

            def linked(t):
                dve.wait_ge(sem["chain"], chain[0] if t is None else val("chain", t, chain[0]))

            def moments(t, name, src, tiles):
                for i in tiles:
                    link(t, nc.vector.bn_stats(st6[name][:, i, :], src(i)))
                linked(t)
                apart()
                for i in tiles:
                    link(t, nc.vector.bn_aggr(mv[name][:, i, :], st6[name][:, i, :]))
                linked(t)

            def normalise(name, dst, src, i):
                return nc.vector.tensor_scalar(dst, src, mv[name][:, i, 0:1], rs[name][:, i:i + 1],
                                               ALU.subtract, ALU.mult)

            def prepare():
                nc.vector.memset(ones[:, :], 1.0).then_inc(s_ones, 1)
                nc.vector.memset(half[:, :], -0.5).then_inc(s_half, 1)
                dve.wait_ge(s_w4, 64)
                def bits(ins):
                    ins.then_inc(s_bits, 1)
                ts = nc.vector.tensor_scalar
                bits(ts(bits1, packed, 0x07070707, 2, ALU.bitwise_and, ALU.logical_shift_left))
                bits(ts(bits2, packed, 0x08080808, 4, ALU.bitwise_and, ALU.logical_shift_left))
                dve.wait_ge(s_bits, 2)
                bits(nc.vector.tensor_tensor(codes[:, 0, :], bits1, bits2, ALU.bitwise_or))
                dve.wait_ge(s_bits, 3)
                bits(ts(bits1, packed, 0x70707070, 2, ALU.bitwise_and, ALU.logical_shift_right))
                bits(ts(bits2, packed, -0x7F7F7F80, None, ALU.bitwise_and))
                dve.wait_ge(s_bits, 5)
                bits(nc.vector.tensor_tensor(codes[:, 1, :], bits1, bits2, ALU.bitwise_or))
                bits(ts(sc32[:, :], sc16[:, :], FP8_SCALE * S_W4, None, ALU.mult))
                dve.wait_ge(s_bits, 7)

                def low(n, dst, src, scale, hi):
                    dve.wait_ge(s_prep_hi, n + 1)
                    nc.vector.scalar_tensor_tensor(dst, src, scale, hi, ALU.mult, ALU.subtract).then_inc(s_prep_lo, 1)

                def dequantise(u):
                    if u >= 4:
                        dve.wait_ge(s_prep_mm, KC + u - 3)
                    for g in range(4):
                        src, k = block_of(u, g)
                        nc.vector.tensor_scalar(wblk[:, u % 4, g, :].rearrange("p (j e) -> p e j", e=2), src,
                                                sc32[:, k:k + 1], None, ALU.mult).then_inc(s_blk_v, 1)

                for c in range(KC):
                    low(c, wq[:, 1, c, :], dense[c][:, :], S_WQ, wq[:, 0, c, :])
                for n, (dst, src, hi) in enumerate(((kup[:, 1, :], raw_kup, kup[:, 0, :]),
                                                    (vup[:, 1, :], raw_vup, vup[:, 0, :]),
                                                    (wkv[:, 1, :, :].rearrange("p a b -> p (a b)"), kf[:, 0:D],
                                                     wkv[:, 0, :, :].rearrange("p a b -> p (a b)")),
                                                    (wo[:, 1, :, :].rearrange("p a b -> p (a b)"), kf[:, D:5 * D],
                                                     wo[:, 0, :, :].rearrange("p a b -> p (a b)")))):
                    dve.wait_ge(s_raw_hi, n + 1)
                    nc.vector.scalar_tensor_tensor(dst, src, S_W, hi, ALU.mult, ALU.subtract).then_inc(s_raw_lo, 1)
                dequantise(1)
                for u in range(UNITS):
                    if u % 2 == 0 and u + 3 < UNITS:
                        dequantise(u + 3)
                    low(KC + u, unit_dst(u, 1), dense[u % 4][:, :].rearrange("p (a b) -> p a b", a=4), 1.0,
                        unit_dst(u, 0))
                dve.wait_ge(sem["xin"], 16)
                moments(None, "ln1", lambda i: xin[:, i, :], range(NT))
                nc.vector.tensor_scalar(ve["ln1"][:, :], mv["ln1"][:, :, 1], EPS, None, ALU.add).then_inc(sem["ve"], 1)
                dve.wait_ge(sem["rs"], 1)
                for i in range(NT):
                    normalise("ln1", xin[:, i, :], xin[:, i, :], i).then_inc(sem["ln1"], 1)

            def step(t, att, ffn, nxt):
                j = jobs(t)
                chain[0] = 0
                n_ve = [0]
                his = {"P1": 0, "C": 4, "Q": 5, "K": 9, "X2": 13 if att else 0}

                def low(kind, i, dst, scale, hi):
                    n = j[kind] + i
                    dve.wait_ge(sem["dense"], val("dense", t, n + 1))
                    dve.wait_ge(sem["hi"], val("hi", t, his[kind] + i + 1))
                    nc.vector.scalar_tensor_tensor(dst, dense[bank(t, n)][:, :], scale, hi, ALU.mult,
                                                   ALU.subtract).then_inc(sem["free"], 1)

                def ask_rstd(name):
                    n_ve[0] += 1
                    scale = {"ln1": 1.0, "ln2": (S_V * S_W) ** 2, "ln3": 1.0}[name]
                    nc.vector.tensor_scalar(ve[name][:, :], mv[name][:, :, 1], EPS * scale, None,
                                            ALU.add).then_inc(sem["ve"], 1)

                def gate(m):
                    n = job_f(t, m, 0)
                    dve.wait_ge(sem["tanh"], val("tanh", t, m + 1))
                    nc.vector.scalar_tensor_tensor(tb[:, m % 2, :], tb[:, m % 2, :], 1.0, dense[bank(t, n)][:, :],
                                                   ALU.add, ALU.mult).then_inc(sem["free"], 1)

                def up(m):
                    n = job_f(t, m, 1)
                    dve.wait_ge(sem["dense"], val("dense", t, n + 1))
                    dve.wait_ge(sem["free"], val("free", t, n))
                    nc.vector.tensor_tensor(tb[:, m % 2, :], tb[:, m % 2, :], dense[bank(t, n)][:, :],
                                            ALU.mult).then_inc(sem["free"], 1)

                def h_low(m):
                    dve.wait_ge(sem["hh"], val("hh", t, m + 1))
                    nc.vector.scalar_tensor_tensor(ht[:, 1, m, :], tb[:, m % 2, :], S_H / (2 * (S_X * S_W4) ** 2),
                                                   ht[:, 0, m, :], ALU.mult, ALU.subtract).then_inc(sem["hl"], 1)

                def o_norm(g):
                    if g > 0:
                        dve.wait_ge(sem["ol"], val("ol", t, g))
                    dve.wait_ge(sem["pv"], val("pv", t, g + 1))
                    link(t, nc.vector.reciprocal(rec[:, :], psSum[:, :]))
                    linked(t)
                    nc.vector.tensor_tensor(rec[:, :], rec[:, :], psO[:, :], ALU.mult).then_inc(sem["on"], 1)

                def o_low(g):
                    dve.wait_ge(sem["oh"], val("oh", t, g + 1))
                    nc.vector.tensor_tensor(ot[:, 1, g, :], rec[:, :], ot[:, 0, g, :],
                                            ALU.subtract).then_inc(sem["ol"], 1)

                def out_tile(i):
                    n = j["D"] + i
                    dve.wait_ge(sem["dense"], val("dense", t, n + 1))
                    dve.wait_ge(sem[f"out{i % 2}"], val(f"out{i % 2}", t, 16 * (i // 2)))
                    moments(t, "lo", lambda i: dense[bank(t, n)][:, :], [i])
                    mean, var, q = mv["lo"][:, i, 0:1], mv["lo"][:, i, 1:2], ve["lo"][:, i:i + 1]
                    link(t, nc.vector.tensor_tensor(q, mean, mean, ALU.mult))
                    linked(t)
                    link(t, nc.vector.tensor_scalar(q, q, EPS, EPS * RMS_EPS * (S_H * S_W4) ** 2, ALU.mult, ALU.add))
                    linked(t)
                    n_ve[0] += 1
                    nc.vector.scalar_tensor_tensor(q, var, 1.0 + EPS, q, ALU.mult, ALU.add).then_inc(sem["ve"], 1)
                    dve.wait_ge(sem["rs"], val("rs", t, n_ve[0]))
                    normalise("lo", stage[:, i % 2, :], dense[bank(t, n)][:, :], i).then_inc(sem["free"], 1)

                if att:
                    for c in range(KC):
                        low("P1", c, xt[:, 1, c, :], S_X, xt[:, 0, c, :])
                if ffn:
                    for i in range(NT):
                        n = j["WO"] + i
                        dve.wait_ge(sem["dense"], val("dense", t, n + 1))
                        nc.vector.tensor_copy(z[:, i, :], dense[bank(t, n)][:, :]).then_inc(sem["free"], 1)
                    dve.wait_ge(sem["free"], val("free", t, j["WO"] + 4))
                    moments(t, "ln2", lambda i: z[:, i, :], range(NT))
                    ask_rstd("ln2")
                if att:
                    low("C", 0, ct[:, 1, :], S_C / (S_X * S_W), ct[:, 0, :])
                if ffn:
                    dve.wait_ge(sem["rs"], val("rs", t, 1))
                    for i in range(NT):
                        normalise("ln2", z[:, i, :], z[:, i, :], i).then_inc(sem["z2"], 1)
                if att:
                    for g in range(NG):
                        low("Q", g, qk[:, 1, g, :], HD ** -0.5 * S_QK / (S_X * S_WQ), qk[:, 0, g, :])
                    for g in range(NG):
                        low("K", g, qk[:, 3, g, :], S_QK / (S_C * S_W), qk[:, 2, g, :])
                if ffn:
                    dve.wait_ge(sem["add2"], val("add2", t, 4))
                    moments(t, "ln3", lambda i: x1[:, i, :], range(NT))
                    ask_rstd("ln3")
                if att:
                    for i in range(NT):
                        n = j["V"] + i
                        dve.wait_ge(sem["dense"], val("dense", t, n + 1))
                        nc.vector.tensor_scalar(v[:, i, :], dense[bank(t, n)][:, :], S_V / (S_C * S_W), None,
                                                ALU.mult).then_inc(sem["free"], 1)
                if ffn:
                    dve.wait_ge(sem["rs"], val("rs", t, 2))
                    for i in range(NT):
                        normalise("ln3", xn2[:, i, :], x1[:, i, :], i).then_inc(sem["ln3"], 1)
                    n_ve[0] = 2
                    for c in range(KC):
                        low("X2", c, x2t[:, 1, c, :], S_X, x2t[:, 0, c, :])
                if not att:
                    for m in range(MI):
                        gate(m)
                        up(m)
                        h_low(m)
                    for i in range(NT):
                        out_tile(i)
                    return
                if isinstance(t, int) and t == 0:
                    dve.wait_ge(s_mask, 2)
                for h in range(H):
                    for i in range(NT):
                        k = NT * h + i
                        dve.wait_ge(sem["mx"], val("mx", t, k + 1))
                        apart()
                        wide = P * (i + 1)
                        nc.vector.tensor_tensor_reduce(out=score[k % 2][:, 0:wide], in0=score[k % 2][:, 0:wide],
                                                       in1=mmax[:, L - wide:L], scale=1.0, scalar=-3e38,
                                                       op0=ALU.add, op1=ALU.max,
                                                       accum_out=mcol[:, k:k + 1]).then_inc(sem["mxfree"], 1)
                    if ffn and h % 3 == 2 and h // 3 < F_EARLY:
                        gate(h // 3)
                    if ffn and h % 3 == 0 and h > 0:
                        up(h // 3 - 1)
                    if ffn and h % 3 == 1 and h > 1:
                        h_low((h - 4) // 3)
                dve.wait_ge(sem["mxfree"], val("mxfree", t, H * NT))
                nc.vector.tensor_scalar(mh[:, :], mcol[:, :], -1.0 / ROW_MAX, None, ALU.mult).then_inc(sem["mh"], 1)
                n = j["MT"]
                dve.wait_ge(sem["dense"], val("dense", t, n + 1))
                nc.vector.tensor_copy(mrow[:, :], dense[bank(t, n)][0:H * NT, 0:P // 2].bitcast(f16)
                                      ).then_inc(sem["free"], 1)
                if ffn:
                    h_low(F_EARLY - 1)
                    gate(F_EARLY)
                    up(F_EARLY)
                for s in range(NG * NT):
                    if s % NT == 0 and s > 0:
                        o_norm(s // NT - 1)
                    if ffn and s % 2 == 1 and 3 <= s <= 11:
                        h_low(F_EARLY + 1 + (s - 3) // 2)
                    if ffn and s == 0:
                        h_low(F_EARLY)
                    if ffn and s % 2 == 1 and s <= 9:
                        gate(F_EARLY + 1 + (s - 1) // 2)
                    if ffn and s % 2 == 0 and 2 <= s <= 10:
                        up(F_EARLY + 1 + (s - 2) // 2)
                    if s % NT == 1 and s > 1:
                        o_low(s // NT - 1)
                    if nxt and s == 3:
                        dve.wait_ge(sem["xin"], val("xin", t, 16))
                        moments(t, "ln1", lambda i: xin[:, i, :], range(NT))
                        ask_rstd("ln1")
                    if nxt and s == 5:
                        dve.wait_ge(sem["rs"], val("rs", t, n_ve[0]))
                        for i in range(NT):
                            normalise("ln1", xin[:, i, :], xin[:, i, :], i).then_inc(sem["ln1"], 1)
                    if ffn and s in (12, 14):
                        out_tile((s - 12) // 2)
                o_norm(NG - 1)
                if ffn:
                    out_tile(2)
                o_low(NG - 1)
                if ffn:
                    out_tile(3)

            prepare()
            step(0, True, False, True)
            with dve.Fori(1, B - 1) as t:
                step(t, True, True, True)
            step(B - 1, True, True, False)
            step(B, False, True, False)

        @block.gpsimd
        def _(pool):
            def power(t, name, k, i0=0, i1=NT):
                pool.wait_ge(sem["ve"], k if t is None else val("ve", t, k))
                nc.gpsimd.tensor_tensor(rs[name][:, i0:i1], ve[name][:, i0:i1], half[:, 0:i1 - i0],
                                        ALU.pow).then_inc(sem["rs"], 1)

            def step(t, att, ffn, nxt):
                k = 0
                if ffn:
                    power(t, "ln2", 1)
                    pool.wait_ge(sem["xres"], val("xres", t, 0))
                    for i in range(NT):
                        pool.wait_ge(sem["z2"], val("z2", t, i + 1))
                        nc.gpsimd.tensor_tensor(x1[:, i, :], x1[:, i, :], z[:, i, :], ALU.add).then_inc(sem["add2"], 1)
                    power(t, "ln3", 2)
                    k = 2
                if nxt:
                    power(t, "ln1", k + 1)
                    k += 1
                if ffn:
                    for i in range(NT):
                        power(t, "lo", k + i + 1, i, i + 1)
                        pool.wait_ge(sem["free"], val("free", t, jobs(t)["D"] + i + 1))
                        nc.gpsimd.tensor_tensor(stage[:, i % 2, :], stage[:, i % 2, :], x1[:, i, :],
                                                ALU.add).then_inc(sem["po"], 1)

            nc.gpsimd.memset(mmax[:, :], 0.0).then_inc(s_mask, 1)
            pool.wait_ge(s_mask, 1)
            nc.gpsimd.affine_select(out=mmax[:, :], in_=mmax[:, :], compare_op=ALU.is_ge, fill=-1e30, base=L - P,
                                    pattern=[[-1, L]], channel_multiplier=1).then_inc(s_mask, 1)
            pool.wait_ge(s_half, 1)
            power(None, "ln1", 1)
            step(0, True, False, True)
            with pool.Fori(1, B - 1) as t:
                step(t, True, True, True)
            step(B - 1, True, True, False)
            step(B, False, True, False)

        @block.sync
        def _(sp):
            rows = lambda a: a.rearrange("(i p) d -> p i d", p=P)

            def step(t, att, ffn, nxt):
                j = jobs(t)
                if nxt:
                    sp.wait_ge(sem["dense"], val("dense", t, j["P1"] + 4))
                    sp.dma_start(xin[:, :, :], rows(x[t + 1, :, :])).then_inc(sem["xin"], 16)
                if att:
                    for last, hi, dst, slots in ((j["Q"] + 4, 0, qst, (0, 1, 0)), (j["K"] + 4, 2, kst, (0, 0, 1))):
                        sp.wait_ge(sem["free"], val("free", t, last))
                        for slot, s in enumerate(slots):
                            for a in range(HG):
                                sp.dma_start(
                                    dst[HD * slot:HD * slot + HD, :, :].rearrange("p (g a) l -> p g a l", a=HG)[:, :, a, :],
                                    qk[HD * a:HD * a + HD, hi + s, :, :]).then_inc(sem["stk"], 16)
                    sp.wait_ge(sem["free"], val("free", t, j["MT"] + 1))
                    sp.dma_start(qst[P - 1:P, :, :].rearrange("p h (i q) -> p (h i) q", q=P),
                                 mrow[:, :]).then_inc(sem["mrow"], 16)
                if ffn:
                    for i in range(NT):
                        sp.wait_ge(sem["po"], val("po", t, i + 1))
                        sp.dma_start(out[t - 1, P * i:P * i + P, :], stage[:, i % 2, :]).then_inc(sem[f"out{i % 2}"], 16)
                        if att:
                            sp.dma_start(x1[:, i, :], x[t, P * i:P * i + P, :]).then_inc(sem["xres"], 16)

            sp.sem_inc(sem["out0"], 16)
            sp.sem_inc(sem["out1"], 16)
            sp.dma_start(raw_wqd, wq_down.rearrange("(r p) d -> p r d", p=P)).then_inc(s_w, 16)
            sp.dma_start(raw_wqu, wq_up_t.rearrange("(r p) d -> p r d", p=P)).then_inc(s_w, 16)
            sp.dma_start(qf[:, 6 * D:8 * D].rearrange("p (a b) -> p a b", a=2)[:, 0, :], k_up_t).then_inc(s_w, 16)
            sp.dma_start(qf[:, 6 * D:8 * D].rearrange("p (a b) -> p a b", a=2)[:, 1, :], v_up_t).then_inc(s_w, 16)
            sp.dma_start(raw_wkv, wkv_down_t.rearrange("(r p) d -> p r d", p=P)).then_inc(s_w, 16)
            sp.dma_start(raw_wo, wo_t.rearrange("(r p) d -> p r d", p=P)).then_inc(s_w, 16)
            for k, (dst, src) in enumerate((
                    (packed[:, 0:GUW].rearrange("p (u w) -> p u w", w=D // 8), gu_packed.rearrange("(u p) w -> p u w", p=P)),
                    (packed[:, GUW:W].rearrange("p (u w) -> p u w", w=I // 8), dn_packed.rearrange("(u p) w -> p u w", p=P)),
                    (sc16[:, 0:2 * MI * GROUPS].rearrange("p (u g) -> p u g", g=GROUPS), gu_scales.rearrange("(u p) g -> p u g", p=P)),
                    (sc16[:, 2 * MI * GROUPS:].rearrange("p (u g) -> p u g", g=MI), dn_scales.rearrange("(u p) g -> p u g", p=P)))):
                sp.dma_start(dst, src).then_inc(s_w4, 16)
            for dst, src in ((tri_sb, tri), (id32, eye32), (id16, eye16), (idbig, eye_big)):
                sp.dma_start(dst[:, :], src).then_inc(s_const, 16)
            sp.dma_start(xin[:, :, :], rows(x[0, :, :])).then_inc(sem["xin"], 16)
            for i in range(NT):
                sp.dma_start(x1[:, i, :], x[0, P * i:P * i + P, :]).then_inc(sem["xres"], 16)
            sp.wait_ge(s_prep_lo, KC)
            sp.wait_ge(s_raw_lo, 4)
            sp.dma_start(qst[96:P - 1, :, :], aug_q[0:HD - 1, :, :]).then_inc(s_aug, 16)
            sp.dma_start(kst[96:P, :, :], aug_k).then_inc(s_aug, 16)
            step(0, True, False, True)
            with sp.Fori(1, B - 1) as t:
                step(t, True, True, True)
            step(B - 1, True, True, False)
            step(B, False, True, False)
            sp.wait_ge(sem["out0"], 16 + 32 * B)
            sp.wait_ge(sem["out1"], 16 + 32 * B)


def constants():
    slopes = np.array([(2.0 ** (-2.0 ** (-(np.log2(H) - 3)))) ** i for i in range(1, H + 1)], np.float32)
    aug_q = np.zeros((HD, H, L), np.float16)
    aug_k = np.zeros((HD, H, L), np.float16)
    pos = np.arange(L, dtype=np.float16)
    left = slopes.astype(np.float64) * S_SCORE
    for n in range(3):
        part = left.astype(np.float16)
        left = left - part
        aug_q[2 * n] = part[:, None]
        aug_k[2 * n] = pos[None]
        aug_q[2 * n + 1] = -pos[None]
        aug_k[2 * n + 1] = part[:, None]
    aug_k[HD - 1] = ROW_MAX
    tri = np.where(np.arange(P)[None] < np.arange(P)[:, None], -60000.0, 0.0).astype(np.float16)
    eye = np.eye(P)
    return {"aug_q": aug_q, "aug_k": aug_k, "tri": tri,
            "eye32": eye.astype(np.float32), "eye16": eye.astype(np.float16), "eye_big": (1024 * eye).astype(np.float16)}


def kernel(L0_attn_hidden_states, L0_attn_Wq_down, L0_attn_Wq_up, L0_attn_Wkv_down, L0_attn_k_up, L0_attn_v_up,
           L0_attn_Wo, L0_ffn_gate_up_packed, L0_ffn_gate_up_scales, L0_ffn_down_packed, L0_ffn_down_scales):
    import concourse.bacc as bacc
    from concourse.bass_utils import run_bass_kernel_spmd
    a = np.asarray
    arrays = {
        "x": a(L0_attn_hidden_states),
        "wq_down": a(L0_attn_Wq_down), "wq_up_t": a(L0_attn_Wq_up).T, "wkv_down_t": a(L0_attn_Wkv_down).T,
        "k_up_t": a(L0_attn_k_up).transpose(1, 0, 2).reshape(RKV, D),
        "v_up_t": a(L0_attn_v_up).transpose(1, 0, 2).reshape(RKV, D),
        "wo_t": a(L0_attn_Wo).T,
        "gu_packed": a(L0_ffn_gate_up_packed), "gu_scales": a(L0_ffn_gate_up_scales).T,
        "dn_packed": a(L0_ffn_down_packed), "dn_scales": a(L0_ffn_down_scales).T,
        **constants(),
    }
    arrays = {n: np.ascontiguousarray(v) for n, v in arrays.items()}
    nc = bacc.Bacc("TRN2", target_bir_lowering=False, num_devices=1)
    aps = {n: nc.dram_tensor(n, v.shape, mybir.dt.from_np(v.dtype), kind="ExternalInput").ap() for n, v in arrays.items()}
    out = nc.dram_tensor("out", (B, L, D), mybir.dt.float32, kind="ExternalOutput").ap()
    nc.disable_value_cache = True
    layer_program(nc, *aps.values(), out)
    r = run_bass_kernel_spmd(nc, [arrays], core_ids=[0])
    return r.results[0]["out"]
```

```python
from contextlib import ExitStack

import concourse.bass as bass
import numpy as np
from concourse import mybir

B, L, D = 16, 512, 512
H, HD = 16, 32
RQ, RKV = 384, 128
I = 1408
P = 128
NT = L // P
KC = D // P
HG = P // HD
NG = H // HG
MI = I // P
GROUPS = D // P
UNITS = 2 * MI + MI

S_X, S_W, S_WQ, S_W4 = 2.0 ** 4, 2.0 ** 8, 2.0 ** 6, 2.0 ** 6
S_C, S_QK, S_V, S_H = 2.0 ** 4, 2.0 ** 4, 2.0 ** 6, 2.0 ** -8
S_SCORE = S_QK * S_QK
ROW_MAX = 1024.0
FP8_SCALE = 2.0 ** 6
EPS, RMS_EPS = 1e-5, 1e-6

COUNTS = {
    "dense": (0, 14, 44, 44), "freev": (0, 9, 31, 31), "freea": (0, 5, 13, 13), "spare": (0, 4, 8, 8),
    "sparefree": (0, 4, 8, 8), "hi": (0, 13, 17, 17),
    "mx": (0, 64, 64, 64), "mxfree": (0, 64, 64, 64), "mh": (0, 1, 1, 1), "mrow": (0, 16, 16, 16),
    "st": (0, 64, 64, 64), "exp": (0, 64, 64, 64), "pv": (0, 4, 4, 4), "sumc": (0, 4, 4, 4), "oc": (0, 4, 4, 4),
    "on": (0, 4, 4, 4), "oh": (0, 4, 4, 4), "ol": (0, 4, 4, 4), "kstk": (0, 192, 192, 192), "qstk0": (0, 192, 192, 192), "qstk1": (0, 192, 192, 192), "xin": (16, 16, 16, 0),
    "xres": (64, 0, 64, 64), "ln1": (4, 4, 4, 0), "ve": (1, 1, 7, 6), "rs": (1, 1, 7, 6),
    "z2": (0, 0, 4, 4), "add2": (0, 0, 4, 4), "ln3": (0, 0, 4, 4), "yn": (0, 0, 4, 4),
    "po": (0, 0, 4, 4), "out0": (16, 0, 32, 32), "out1": (16, 0, 32, 32), "tanh": (0, 0, 11, 11), "hh": (0, 0, 11, 11),
    "hl": (0, 0, 11, 11), "chain": (8, 12, 44, 36),
}
F_EARLY = 9
ATT_JOBS = {"C": 0, "Q": 1, "K": 2, "Q1": 6, "V": 9, "MT": 13}
BOTH_JOBS = {"WO": 0, "C": 4, "Q": 5, "K": 6, "Q1": 10, "V": 13, "F": 17, "MT": 17 + 2 * F_EARLY + 1, "F2": 17 + 2 * F_EARLY + 2,
             "D": 18 + 2 * MI}
FFN_JOBS = {"WO": 0, "F": 4, "D": 4 + 2 * MI}
TAKES = {"WO": "a", "C": "v", "Q": "v", "K": "v", "Q1": "v", "V": "a", "F": "v", "MT": "a", "F2": "v", "D": "a"}

SLOTS = 2 * H
GU_PRODUCTS = 3 * KC
D_PRODUCTS = 3 * MI
D_FIRST = 18
F_FIRST = 18
D_TAIL = 12
LN1_SLOT = 13
LATE = MI - F_EARLY - 1
SLOT_WEIGHTS = (9, 7, 5, 4)


def mx_cut(slot):
    return F_FIRST + (2 * F_EARLY * GU_PRODUCTS - F_FIRST) * slot // SLOTS


def mx_done(q):
    return next((s for s in range(SLOTS) if mx_cut(s + 1) >= GU_PRODUCTS * (q + 1)), SLOTS) if q * GU_PRODUCTS >= F_FIRST else -1


def exp_cut(slot):
    n = 2 * LATE * GU_PRODUCTS + NT * D_PRODUCTS - D_TAIL
    weight = [SLOT_WEIGHTS[s // 2 % NT] for s in range(SLOTS)]
    return n * sum(weight[:slot]) // sum(weight)


def exp_done(products):
    return next((s for s in range(SLOTS) if exp_cut(s + 1) >= products), SLOTS)


def late_done(m, up):
    return exp_done(GU_PRODUCTS * (2 * (m - F_EARLY - 1) + up + 1))


def down_done(i):
    n = 2 * LATE * GU_PRODUCTS
    return exp_done(n + (D_PRODUCTS + D_FIRST, 2 * D_PRODUCTS, 3 * D_PRODUCTS, 4 * D_PRODUCTS)[i])


def layer_program(nc, x, wq_down, wq_up_t, wkv_down_t, k_up_t, v_up_t, wo_t, gu_packed, gu_scales,
                  dn_packed, dn_scales, aug_q, aug_k, tri, eye32, eye16, eye_big, out):
    f32, f16, bf16 = mybir.dt.float32, mybir.dt.float16, mybir.dt.bfloat16
    i32, fp8 = mybir.dt.int32, mybir.dt.float8e4
    ACT, ALU = mybir.ActivationFunctionType, mybir.AluOpType

    ctx = ExitStack()
    with ctx:
        def sb(name, shape, dt):
            return ctx.enter_context(nc.sbuf_tensor(name, shape, dt))

        wq = sb("wq", [P, 2, KC, D], f16)
        wkv = sb("wkv", [P, 2, KC, RKV], f16)
        kup = sb("kup", [P, 2, D], f16)
        vup = sb("vup", [P, 2, D], f16)
        wo = sb("wo", [P, 2, KC, D], f16)
        wgu = sb("wgu", [P, 2, KC, 2 * I], f16)
        wdn = sb("wdn", [P, 2, MI, D], f16)
        xin = sb("xin", [P, NT, D], f32)
        x1 = sb("x1", [P, NT, D], f32)
        stage = sb("stage", [P, 2, D], f32)
        tb = sb("tb", [P, 2, L], f32)
        rec = sb("rec", [P, L], f32)
        osb = sb("osb", [P, L], f32)
        ct = sb("ct", [P, 2, L], f16)
        qst = sb("qst", [P, H, L], f16)
        kst = sb("kst", [P, H, L], f16)
        HT0 = NT * D
        P0 = HT0 + 2 * MI * L // 2
        O0 = P0 + HG * L
        X20 = O0 + 2 * KC * L // 2
        arena = sb("arena", [P, X20 + 2 * KC * L // 2], f32)
        v = arena[:, 0:HT0].rearrange("p (a b) -> p a b", a=NT)
        z = v
        ht = arena[:, HT0:P0].bitcast(f16).rearrange("p (s a b) -> p s a b", s=2, a=MI)
        qk = arena[:, HT0:HT0 + 4 * NG * L // 2].bitcast(f16).rearrange("p (s a b) -> p s a b", s=4, a=NG)
        prob = arena[:, P0:O0].rearrange("p (a b) -> p a b", a=HG)
        xt = arena[:, P0:O0].bitcast(f16).rearrange("p (s a b) -> p s a b", s=2, a=KC)
        ot = arena[:, O0:X20].bitcast(f16).rearrange("p (s a b) -> p s a b", s=2, a=NG)
        xn2 = arena[:, O0:X20].rearrange("p (a b) -> p a b", a=NT)
        x2t = arena[:, X20:X20 + KC * L].bitcast(f16).rearrange("p (s a b) -> p s a b", s=2, a=KC)
        GUW, DNW = 2 * MI * (D // 8), KC * (I // 8)
        W = GUW + DNW
        packed = arena[:, 0:W].bitcast(i32)
        bits1 = arena[:, W:2 * W].bitcast(i32)
        bits2 = arena[:, 2 * W:3 * W].bitcast(i32)
        codes = arena[:, 3 * W:5 * W].bitcast(i32).rearrange("p (e w) -> p e w", e=2)
        codes8 = arena[:, 3 * W:5 * W].bitcast(fp8).rearrange("p (e w) -> p e w", e=2)
        wblk = arena[:, 5 * W:5 * W + 4 * D].rearrange("p (r a b) -> p r a b", r=4, a=4)
        qf = qst[:, :, :].rearrange("p a b -> p (a b)").bitcast(f32)
        kf = kst[:, :, :].rearrange("p a b -> p (a b)").bitcast(f32)
        raw_wqd = qf[:, 0:3 * D].rearrange("p (a b) -> p a b", a=3)
        raw_wqu = qf[:, 3 * D:6 * D].rearrange("p (a b) -> p a b", a=3)
        raw_kup = qf[:, 6 * D:7 * D]
        raw_vup = qf[:, 7 * D:8 * D]
        raw_wkv = kf[:, 0:D].rearrange("p (a b) -> p a b", a=KC)
        raw_wo = kf[:, D:5 * D].rearrange("p (a b) -> p a b", a=KC)
        SC0, NSC = 5 * W + 4 * D, 2 * MI * GROUPS + KC * MI
        sc16 = arena[:, SC0:SC0 + NSC // 2].bitcast(f16)
        sc32 = arena[:, SC0 + NSC // 2:SC0 + NSC // 2 + NSC]
        mmax = sb("mmax", [P, L], bf16)
        tri_sb = sb("tri_sb", [P, P], f16)
        id32 = sb("id32", [P, P], f32)
        id16 = sb("id16", [P, P], f16)
        idbig = sb("idbig", [P, P], f16)
        ones = sb("ones", [P, HD], f32)
        mcol = sb("mcol", [P, H * NT], f32)
        mh = sb("mh", [P, H * NT], f16)
        mrow = sb("mrow", [H * NT, P], f16)
        half = sb("half", [P, NT], f32)
        st6 = {n: sb("st6_" + n, [P, NT, 6], f32) for n in ("ln1", "ln2", "ln3", "lo")}
        mv = {n: sb("mv_" + n, [P, NT, 2], f32) for n in ("ln1", "ln2", "ln3", "lo")}
        ve = {n: sb("ve_" + n, [P, NT], f32) for n in ("ln1", "ln2", "ln3", "lo")}
        rs = {n: sb("rs_" + n, [P, NT], f32) for n in ("ln1", "ln2", "ln3", "lo")}

        def ps(name):
            return ctx.enter_context(nc.psum_tensor(name, [P, 512], f32))
        dense = [ps(f"dense{i}") for i in range(4)]
        score = [ps(f"score{i}") for i in range(2)]
        psO, psSum = ps("psO"), ps("psSum")
        spare = [score[0], score[1], psO, psSum]

        sem = {n: ctx.enter_context(nc.semaphore("s_" + n)) for n in COUNTS}
        s_w = ctx.enter_context(nc.semaphore("s_w"))
        s_w4 = ctx.enter_context(nc.semaphore("s_w4"))
        s_const = ctx.enter_context(nc.semaphore("s_const"))
        s_aug = ctx.enter_context(nc.semaphore("s_aug"))
        s_passed_v = ctx.enter_context(nc.semaphore("s_passed_v"))
        s_passed_t = ctx.enter_context(nc.semaphore("s_passed_t"))
        s_mask = ctx.enter_context(nc.semaphore("s_mask"))
        s_ones = ctx.enter_context(nc.semaphore("s_ones"))
        s_half = ctx.enter_context(nc.semaphore("s_half"))
        s_bits = ctx.enter_context(nc.semaphore("s_bits"))
        s_prep_mm = ctx.enter_context(nc.semaphore("s_prep_mm"))
        s_prep_hi = ctx.enter_context(nc.semaphore("s_prep_hi"))
        s_prep_lo = ctx.enter_context(nc.semaphore("s_prep_lo"))
        s_raw_hi = ctx.enter_context(nc.semaphore("s_raw_hi"))
        s_raw_lo = ctx.enter_context(nc.semaphore("s_raw_lo"))
        s_blk_a = ctx.enter_context(nc.semaphore("s_blk_a"))
        s_blk_v = ctx.enter_context(nc.semaphore("s_blk_v"))

        def val(name, t, k):
            pre, n0, nb, n_last = COUNTS[name]
            if isinstance(t, int) and t == 0:
                return pre + k
            if isinstance(t, int) and t == B:
                return pre + n0 + nb * (B - 2) + n_last + k
            return nb * t + (pre + n0 - nb + k)

        def jobs(t):
            if isinstance(t, int) and t == 0:
                return ATT_JOBS
            return FFN_JOBS if isinstance(t, int) and t == B else BOTH_JOBS

        def job_f(t, m, up):
            q, j = 2 * m + up, jobs(t)
            return j["F2"] + q - 2 * F_EARLY - 1 if "F2" in j and q > 2 * F_EARLY else j["F"] + q

        def job_q(t, g):
            return jobs(t)["Q"] if g == 0 else jobs(t)["Q1"] + g - 1

        def taken(eng, t, n):
            j = jobs(t)
            kind_of = lambda n: max((k for k in j if j[k] <= n), key=lambda k: j[k])
            who = TAKES[kind_of(n)] if n >= 0 else "a"
            count = sum(1 for i in range(n + 1) if TAKES[kind_of(i)] == who) if n >= 0 else n + 1
            eng.wait_ge(sem["free" + who], val("free" + who, t, count))

        def bank(t, n):
            pre, n0, nb, n_last = COUNTS["dense"]
            start = 0 if isinstance(t, int) and t == 0 else n0
            return (start + n) % 4

        def terms(w, a, n):
            out_ = []
            for c in range(n):
                out_ += [(w(0, c), a(0, c)), (w(0, c), a(1, c)), (w(1, c), a(0, c))]
            return out_

        def block_of(u, g):
            if u < 2 * MI:
                w0, k = (D // 8) * u + 16 * g, GROUPS * u + g
            else:
                m = u - 2 * MI
                w0, k = GUW + (I // 8) * g + 16 * m, 2 * MI * GROUPS + MI * g + m
            return codes8[:, :, 4 * w0:4 * w0 + 64], k

        def unit_dst(u, s):
            if u < 2 * MI:
                return wgu[:, s, :, P * u:P * u + P]
            return wdn[:, s, u - 2 * MI, :].rearrange("p (a b) -> p a b", a=4)

        block = ctx.enter_context(nc.Block())

        @block.tensor
        def _(pe):
            def open_job(t, n):
                if isinstance(t, int) and t == 0 and n < 4:
                    return
                taken(pe, t, n - 4)

            def products(dst, tt, first=True, last=True):
                for k, (w, a) in enumerate(tt):
                    ins = nc.tensor.matmul(dst, w, a, start=first and k == 0, stop=last and k == len(tt) - 1)
                return ins

            def transposes(c, src):
                for i in range(NT):
                    ins = nc.tensor.transpose(spare[c][:, P * i:P * i + P], src(i), id32[:, :])
                ins.then_inc(sem["spare"], 1)

            def prepare():
                pe.wait_ge(s_const, 64)
                pe.wait_ge(s_ones, 1)
                pe.wait_ge(s_w, 96)
                for c in range(KC):
                    for r in range(3):
                        ins = nc.tensor.matmul(dense[c][:, :], raw_wqd[:, r, P * c:P * c + P], raw_wqu[:, r, :],
                                               start=r == 0, stop=r == 2)
                    ins.then_inc(s_prep_mm, 1)
                for u in range(UNITS):
                    pe.wait_ge(s_prep_lo, u + 1)
                    pe.wait_ge(s_blk_v if u % 2 else s_blk_a, 4 * (u // 2) + 4)
                    for g in range(4):
                        ins = nc.tensor.transpose(dense[u % 4][:, P * g:P * g + P], wblk[:, u % 4, g, :], id32[:, :])
                    ins.then_inc(s_prep_mm, 1)
                pe.wait_ge(s_prep_lo, KC + UNITS)
                pe.wait_ge(s_raw_lo, 4)

            def step(t, att, ffn, nxt):
                j = jobs(t)
                if att:
                    pe.wait_ge(sem["ln1"], val("ln1", t, 0) if not (isinstance(t, int) and t == 0) else 4)
                    for c in range(KC):
                        if c == 2 and ffn:
                            pe.wait_ge(sem["oc"], val("oc", t, 0))
                        transposes(c, lambda i: xin[:, i, P * c:P * c + P])
                if ffn:
                    for part, (lo, hi) in enumerate(((0, 3 * (NG - 1)), (3 * (NG - 1), 3 * NG))):
                        pe.wait_ge(sem["ol"], val("ol", t, part - 1))
                        for i in range(NT):
                            n = j["WO"] + i
                            if part == 0:
                                open_job(t, n)
                            tt = terms(lambda s, c: ot[:, s, c, P * i:P * i + P], lambda s, c: wo[:, s, c, :], NG)
                            ins = products(dense[bank(t, n)][:, :], tt[lo:hi], part == 0, part == 1)
                            if part == 1:
                                ins.then_inc(sem["dense"], 1)
                if att:
                    pe.wait_ge(sem["sparefree"], val("sparefree", t, 4))
                    open_job(t, j["C"])
                    products(dense[bank(t, j["C"])][:, :],
                             terms(lambda s, c: wkv[:, s, c, :], lambda s, c: xt[:, s, c, :], KC)
                             ).then_inc(sem["dense"], 1)
                    def job_products_q(g):
                        n = job_q(t, g)
                        open_job(t, n)
                        products(dense[bank(t, n)][:, :],
                                 terms(lambda s, c: wq[:, s, c, P * g:P * g + P], lambda s, c: xt[:, s, c, :], KC)
                                 ).then_inc(sem["dense"], 1)

                    job_products_q(0)
                    taken(pe, t, j["C"])
                    for g in range(NG):
                        open_job(t, j["K"] + g)
                        products(dense[bank(t, j["K"] + g)][:, :],
                                 terms(lambda s, c: kup[:, s, P * g:P * g + P], lambda s, c: ct[:, s, :], 1)
                                 ).then_inc(sem["dense"], 1)
                    for g in range(1, NG):
                        job_products_q(g)
                    for i in range(NT):
                        open_job(t, j["V"] + i)
                        products(dense[bank(t, j["V"] + i)][:, :],
                                 terms(lambda s, c: ct[:, s, P * i:P * i + P], lambda s, c: vup[:, s, :], 1)
                                 ).then_inc(sem["dense"], 1)
                if ffn:
                    for i in range(NT):
                        pe.wait_ge(sem["ln3"], val("ln3", t, i + 1))
                        for c in range(KC):
                            ins = nc.tensor.transpose(spare[c][:, P * i:P * i + P], xn2[:, i, P * c:P * c + P],
                                                      id32[:, :])
                            if i == NT - 1:
                                ins.then_inc(sem["spare"], 1)

                def ffn_up(m, up, a, b):
                    n = job_f(t, m, up)
                    if a == 0:
                        open_job(t, n)
                    col = I * up + P * m
                    tt = terms(lambda s, c: wgu[:, s, c, col:col + P], lambda s, c: x2t[:, s, c, :], KC)
                    for c in range(KC if m == 0 and not up else 0):
                        pe.wait_ge(sem["sparefree"], val("sparefree", t, (4 if att else 0) + c + 1))
                        products(dense[bank(t, n)][:, :], tt[3 * c:3 * c + 2], c == 0, False)
                        ins = products(dense[bank(t, n)][:, :], tt[3 * c + 2:3 * c + 3], False, c == KC - 1)
                    if m or up:
                        ins = products(dense[bank(t, n)][:, :], tt[a:b], a == 0, b == GU_PRODUCTS)
                    if b == GU_PRODUCTS:
                        ins.then_inc(sem["dense"], 1)

                def ffn_down(i, a, b):
                    n = j["D"] + i
                    if a == 0:
                        open_job(t, n)
                    tt = terms(lambda s, m: ht[:, s, m, P * i:P * i + P], lambda s, m: wdn[:, s, m, :], MI)
                    pe.wait_ge(sem["hl"], val("hl", t, (b + 2) // 3))
                    ins = products(dense[bank(t, n)][:, :], tt[a:b], a == 0, b == D_PRODUCTS)
                    if b == D_PRODUCTS:
                        ins.then_inc(sem["dense"], 1)

                def run_early(a, b):
                    for q in range(2 * F_EARLY):
                        lo, hi = max(a, GU_PRODUCTS * q), min(b, GU_PRODUCTS * (q + 1))
                        if lo < hi:
                            ffn_up(q // 2, q % 2, lo - GU_PRODUCTS * q, hi - GU_PRODUCTS * q)

                def run_late(a, b):
                    start = 0
                    for r in range(2 * LATE):
                        lo, hi = max(a, start), min(b, start + GU_PRODUCTS)
                        if lo < hi:
                            ffn_up(F_EARLY + 1 + r // 2, r % 2, lo - start, hi - start)
                        start += GU_PRODUCTS
                    for i, first, last in ((0, 0, D_FIRST), (1, 0, D_FIRST), (0, D_FIRST, D_PRODUCTS),
                                           (1, D_FIRST, D_PRODUCTS), (2, 0, D_PRODUCTS), (3, 0, D_PRODUCTS)):
                        lo, hi = max(a, start), min(b, start + last - first)
                        if lo < hi:
                            ffn_down(i, first + lo - start, first + hi - start)
                        start += last - first

                if not att:
                    for m in range(MI):
                        ffn_up(m, 0, 0, 12)
                        ffn_up(m, 1, 0, 12)
                    for i in range(NT):
                        ffn_down(i, 0, D_PRODUCTS)
                    return
                if ffn:
                    run_early(0, mx_cut(0))
                if isinstance(t, int) and t == 0:
                    pe.wait_ge(s_aug, 32)
                pe.wait_ge(sem["kstk"], val("kstk", t, 192))
                pe.wait_ge(sem["qstk0"], val("qstk0", t, 192))
                for h in range(H):
                    for i in range(NT):
                        k = NT * h + i
                        if k == NT * H // 2:
                            pe.wait_ge(sem["qstk1"], val("qstk1", t, 192))
                        if k >= 2:
                            pe.wait_ge(sem["mxfree"], val("mxfree", t, k - 1))
                        nc.tensor.matmul(score[k % 2][:, 0:P * (i + 1)], qst[0:P - 1, h, P * i:P * i + P],
                                         kst[0:P - 1, h, 0:P * (i + 1)], start=True, stop=True).then_inc(sem["mx"], 1)
                        if ffn and i % 2 == 1:
                            run_early(mx_cut(k // 2), mx_cut(k // 2 + 1))
                if ffn:
                    ffn_up(F_EARLY, 0, 0, GU_PRODUCTS)
                pe.wait_ge(sem["mh"], val("mh", t, 1))
                open_job(t, j["MT"])
                pe.sem_inc(s_passed_t, 1)
                nc.tensor.transpose(dense[bank(t, j["MT"])][0:H * NT, 0:P // 2].bitcast(f16), mh[:, :],
                                    id16[:, :]).then_inc(sem["dense"], 1)
                if ffn:
                    ffn_up(F_EARLY, 1, 0, GU_PRODUCTS)
                pe.wait_ge(sem["mrow"], val("mrow", t, 16))

                for s in range(NG * NT):
                    g, kt = s // NT, s % NT
                    wide = L - P * kt
                    for a in range(HG):
                        h, e = HG * g + a, HG * s + a
                        if e >= 2:
                            pe.wait_ge(sem["exp"], val("exp", t, e - 1))
                        nc.tensor.matmul(score[e % 2][:, 0:wide], kst[:, h, P * kt:P * kt + P],
                                         qst[:, h, P * kt:L], start=True, stop=False)
                        nc.tensor.matmul(score[e % 2][:, 0:P], idbig[:, :], tri_sb[:, :],
                                         start=False, stop=True).then_inc(sem["st"], 1)
                        if ffn and a % 2 == 1:
                            run_late(exp_cut(e // 2), exp_cut(e // 2 + 1))
                    pe.wait_ge(sem["exp"], val("exp", t, HG * s + HG))
                    if kt == 0 and g > 0:
                        pe.wait_ge(sem["oc"], val("oc", t, g))
                    for a in range(HG):
                        nc.tensor.matmul(psO[HD * a:HD * a + HD, P * kt:L], v[:, kt, HD * (HG * g + a):HD * (HG * g + a) + HD],
                                         prob[:, a, 0:wide], start=kt == 0, stop=kt == NT - 1)
                    for a in range(HG):
                        ins = nc.tensor.matmul(psSum[HD * a:HD * a + HD, P * kt:L], ones[:, :],
                                               prob[:, a, 0:wide], start=kt == 0, stop=kt == NT - 1)
                    if kt == NT - 1:
                        ins.then_inc(sem["pv"], 1)
                if ffn:
                    run_late(exp_cut(SLOTS), exp_cut(SLOTS) + D_TAIL)

            prepare()
            step(0, True, False, True)
            with pe.Fori(1, B - 1) as t:
                step(t, True, True, True)
            step(B - 1, True, True, False)
            step(B, False, True, False)

        @block.scalar
        def _(act):
            def prepare():
                act.wait_ge(s_w, 96)
                for n, (dst, src) in enumerate(((kup[:, 0, :], raw_kup), (vup[:, 0, :], raw_vup),
                                                (wkv[:, 0, :, :], raw_wkv), (wo[:, 0, :, :], raw_wo))):
                    nc.scalar.activation(dst, src, ACT.Copy, scale=S_W).then_inc(s_raw_hi, 1)

                def dequantise(u):
                    act.wait_ge(s_bits, 7)
                    if u >= 4:
                        act.wait_ge(s_prep_mm, KC + u - 3)
                    for g in range(4):
                        src, k = block_of(u, g)
                        nc.scalar.activation(wblk[:, u % 4, g, :].rearrange("p (j e) -> p e j", e=2), src, ACT.Copy,
                                             scale=sc32[:, k:k + 1]).then_inc(s_blk_a, 1)

                def high(n, dst, src, scale):
                    act.wait_ge(s_prep_mm, n + 1)
                    nc.scalar.activation(dst, src, ACT.Copy, scale=scale).then_inc(s_prep_hi, 1)

                for c in range(KC):
                    high(c, wq[:, 0, c, :], dense[c][:, :], S_WQ)
                dequantise(0)
                for u in range(UNITS):
                    if u % 2 == 1 and u + 1 < UNITS:
                        dequantise(u + 1)
                    high(KC + u, unit_dst(u, 0), dense[u % 4][:, :].rearrange("p (a b) -> p a b", a=4), 1.0)

            def step(t, att, ffn, nxt):
                j = jobs(t)
                n_spare = [0]

                def high(n, dst, scale):
                    act.wait_ge(sem["dense"], val("dense", t, n + 1))
                    nc.scalar.activation(dst, dense[bank(t, n)][:, :], ACT.Copy, scale=scale).then_inc(sem["hi"], 1)

                def high_spare(c, dst, scale):
                    n_spare[0] += 1
                    act.wait_ge(sem["spare"], val("spare", t, n_spare[0]))
                    nc.scalar.activation(dst, spare[c][:, :], ACT.Copy, scale=scale).then_inc(sem["hi"], 1)

                def tanh(m):
                    if m >= 2:
                        act.wait_ge(sem["hl"], val("hl", t, m - 1))
                    n = job_f(t, m, 0)
                    act.wait_ge(sem["dense"], val("dense", t, n + 1))
                    nc.scalar.activation(tb[:, m % 2, :], dense[bank(t, n)][:, :], ACT.Tanh,
                                         scale=0.5 / (S_X * S_W4)).then_inc(sem["tanh"], 1)

                def h_high(m):
                    taken(act, t, job_f(t, m, 1))
                    nc.scalar.activation(ht[:, 0, m, :], tb[:, m % 2, :], ACT.Copy).then_inc(sem["hh"], 1)

                def o_copy(g):
                    act.wait_ge(sem["pv"], val("pv", t, g + 1))
                    if ffn or g > 0:
                        act.wait_ge(sem["ol"], val("ol", t, g))
                    nc.scalar.activation(rec[:, :], psSum[:, :], ACT.Copy).then_inc(sem["sumc"], 1)
                    nc.scalar.activation(osb[:, :], psO[:, :], ACT.Copy).then_inc(sem["oc"], 1)

                def o_high(g):
                    act.wait_ge(sem["on"], val("on", t, g + 1))
                    nc.scalar.activation(ot[:, 0, g, :], rec[:, :], ACT.Copy).then_inc(sem["oh"], 1)

                def y_copy(i):
                    n = j["D"] + i
                    act.wait_ge(sem["dense"], val("dense", t, n + 1))
                    act.wait_ge(sem[f"out{i % 2}"], val(f"out{i % 2}", t, 16 * (i // 2)))
                    nc.scalar.activation(stage[:, i % 2, :], dense[bank(t, n)][:, :], ACT.Copy).then_inc(sem["freea"], 1)

                if att:
                    for c in range(KC):
                        high_spare(c, xt[:, 0, c, :], S_X)
                if ffn:
                    for i in range(NT):
                        n = j["WO"] + i
                        act.wait_ge(sem["dense"], val("dense", t, n + 1))
                        nc.scalar.activation(z[:, i, :], dense[bank(t, n)][:, :], ACT.Copy).then_inc(sem["freea"], 1)
                if att:
                    high(j["C"], ct[:, 0, :], S_C / (S_X * S_W))
                    high(job_q(t, 0), qk[:, 0, 0, :], HD ** -0.5 * S_QK / (S_X * S_WQ))
                    for g in range(NG):
                        high(j["K"] + g, qk[:, 2, g, :], S_QK / (S_C * S_W))
                    for g in range(1, NG):
                        high(job_q(t, g), qk[:, 0, g, :], HD ** -0.5 * S_QK / (S_X * S_WQ))
                    if ffn:
                        act.wait_ge(sem["add2"], val("add2", t, 4))
                    for i in range(NT):
                        n = j["V"] + i
                        act.wait_ge(sem["dense"], val("dense", t, n + 1))
                        nc.scalar.activation(v[:, i, :], dense[bank(t, n)][:, :], ACT.Copy,
                                             scale=S_V / (S_C * S_W)).then_inc(sem["freea"], 1)
                if ffn:
                    for c in range(KC):
                        high_spare(c, x2t[:, 0, c, :], S_X)
                if not att:
                    for m in range(MI):
                        tanh(m)
                        h_high(m)
                    for i in range(NT):
                        y_copy(i)
                    return
                if ffn:
                    tanh(0)
                    act.wait_ge(sem["qstk1"], val("qstk1", t, 192))
                    h_high(0)
                    for m in range(1, F_EARLY):
                        tanh(m)
                        h_high(m)
                n = j["MT"]
                act.wait_ge(sem["dense"], val("dense", t, n + 1))
                nc.scalar.activation(mrow[:, :], dense[bank(t, n)][0:H * NT, 0:P // 2].bitcast(f16), ACT.Copy
                                     ).then_inc(sem["freea"], 1)
                if ffn:
                    tanh(F_EARLY)
                    h_high(F_EARLY)
                for e in range(HG * NG * NT):
                    s, slot = e // HG, e // 2
                    wide = L - P * (s % NT)
                    act.wait_ge(sem["st"], val("st", t, e + 1))
                    nc.scalar.activation(prob[:, e % HG, 0:wide], score[e % 2][:, 0:wide], ACT.Exp,
                                         scale=1.0 / S_SCORE).then_inc(sem["exp"], 1)
                    if e % 2 == 0:
                        continue
                    if slot % (2 * NT) == 0 and slot > 0:
                        o_copy(slot // (2 * NT) - 1)
                    if slot % (2 * NT) == 3 and slot > 2 * NT:
                        o_high(slot // (2 * NT) - 1)
                    if ffn:
                        for m in range(F_EARLY + 1, MI):
                            if slot == late_done(m, 0) + 1:
                                tanh(m)
                            if slot == late_done(m, 1) + 2:
                                h_high(m)
                        for i in range(NT):
                            if slot == down_done(i) + 1:
                                y_copy(i)
                o_copy(NG - 1)
                if ffn:
                    for i in range(NT):
                        if down_done(i) + 1 >= SLOTS:
                            y_copy(i)
                o_high(NG - 1)

            prepare()
            step(0, True, False, True)
            with act.Fori(1, B - 1) as t:
                step(t, True, True, True)
            step(B - 1, True, True, False)
            step(B, False, True, False)

        @block.vector
        def _(dve):
            chain = [0]

            def link(t, ins):
                chain[0] += 1
                ins.then_inc(sem["chain"], 1)

            def apart():
                dve.sem_inc(s_passed_v, 1)

            def linked(t):
                dve.wait_ge(sem["chain"], chain[0] if t is None else val("chain", t, chain[0]))

            def moments(t, name, src, tiles, ready=None):
                for i in tiles:
                    if ready:
                        ready(i)
                    link(t, nc.vector.bn_stats(st6[name][:, i, :], src(i)))
                linked(t)
                apart()
                for i in tiles:
                    link(t, nc.vector.bn_aggr(mv[name][:, i, :], st6[name][:, i, :]))
                linked(t)

            def normalise(name, dst, src, i):
                return nc.vector.tensor_scalar(dst, src, mv[name][:, i, 0:1], rs[name][:, i:i + 1],
                                               ALU.subtract, ALU.mult)

            def prepare():
                nc.vector.memset(ones[:, :], 1.0).then_inc(s_ones, 1)
                nc.vector.memset(half[:, :], -0.5).then_inc(s_half, 1)
                dve.wait_ge(s_w4, 64)
                def bits(ins):
                    ins.then_inc(s_bits, 1)
                ts = nc.vector.tensor_scalar
                bits(ts(bits1, packed, 0x07070707, 2, ALU.bitwise_and, ALU.logical_shift_left))
                bits(ts(bits2, packed, 0x08080808, 4, ALU.bitwise_and, ALU.logical_shift_left))
                dve.wait_ge(s_bits, 2)
                bits(nc.vector.tensor_tensor(codes[:, 0, :], bits1, bits2, ALU.bitwise_or))
                dve.wait_ge(s_bits, 3)
                bits(ts(bits1, packed, 0x70707070, 2, ALU.bitwise_and, ALU.logical_shift_right))
                bits(ts(bits2, packed, -0x7F7F7F80, None, ALU.bitwise_and))
                dve.wait_ge(s_bits, 5)
                bits(nc.vector.tensor_tensor(codes[:, 1, :], bits1, bits2, ALU.bitwise_or))
                bits(ts(sc32, sc16, FP8_SCALE * S_W4, None, ALU.mult))
                dve.wait_ge(s_bits, 7)

                def low(n, dst, src, scale, hi):
                    dve.wait_ge(s_prep_hi, n + 1)
                    nc.vector.scalar_tensor_tensor(dst, src, scale, hi, ALU.mult, ALU.subtract).then_inc(s_prep_lo, 1)

                def dequantise(u):
                    if u >= 4:
                        dve.wait_ge(s_prep_mm, KC + u - 3)
                    for g in range(4):
                        src, k = block_of(u, g)
                        nc.vector.tensor_scalar(wblk[:, u % 4, g, :].rearrange("p (j e) -> p e j", e=2), src,
                                                sc32[:, k:k + 1], None, ALU.mult).then_inc(s_blk_v, 1)

                for c in range(KC):
                    low(c, wq[:, 1, c, :], dense[c][:, :], S_WQ, wq[:, 0, c, :])
                for n, (dst, src, hi) in enumerate(((kup[:, 1, :], raw_kup, kup[:, 0, :]),
                                                    (vup[:, 1, :], raw_vup, vup[:, 0, :]),
                                                    (wkv[:, 1, :, :].rearrange("p a b -> p (a b)"), kf[:, 0:D],
                                                     wkv[:, 0, :, :].rearrange("p a b -> p (a b)")),
                                                    (wo[:, 1, :, :].rearrange("p a b -> p (a b)"), kf[:, D:5 * D],
                                                     wo[:, 0, :, :].rearrange("p a b -> p (a b)")))):
                    dve.wait_ge(s_raw_hi, n + 1)
                    nc.vector.scalar_tensor_tensor(dst, src, S_W, hi, ALU.mult, ALU.subtract).then_inc(s_raw_lo, 1)
                dequantise(1)
                for u in range(UNITS):
                    if u % 2 == 0 and u + 3 < UNITS:
                        dequantise(u + 3)
                    low(KC + u, unit_dst(u, 1), dense[u % 4][:, :].rearrange("p (a b) -> p a b", a=4), 1.0,
                        unit_dst(u, 0))
                dve.wait_ge(sem["xin"], 16)
                moments(None, "ln1", lambda i: xin[:, i, :], range(NT))
                nc.vector.tensor_scalar(ve["ln1"][:, :], mv["ln1"][:, :, 1], EPS, None, ALU.add).then_inc(sem["ve"], 1)
                dve.wait_ge(sem["rs"], 1)
                for i in range(NT):
                    normalise("ln1", xin[:, i, :], xin[:, i, :], i).then_inc(sem["ln1"], 1)

            def step(t, att, ffn, nxt):
                j = jobs(t)
                chain[0] = 0
                n_ve = [0]
                n_spare = [0]
                his = {"P1": 0, "C": 4, "Q": 5, "K": 6, "Q1": 10, "X2": 13 if att else 0}

                def low(kind, i, dst, scale, hi):
                    if kind in ("P1", "X2"):
                        n_spare[0] += 1
                        dve.wait_ge(sem["spare"], val("spare", t, n_spare[0]))
                        src, done = spare[i], sem["sparefree"]
                    else:
                        n = j[kind] + i
                        dve.wait_ge(sem["dense"], val("dense", t, n + 1))
                        src, done = dense[bank(t, n)], sem["freev"]
                    dve.wait_ge(sem["hi"], val("hi", t, his[kind] + i + 1))
                    nc.vector.scalar_tensor_tensor(dst, src[:, :], scale, hi, ALU.mult, ALU.subtract).then_inc(done, 1)

                def ask_rstd(name):
                    n_ve[0] += 1
                    scale = {"ln1": 1.0, "ln2": (S_V * S_W) ** 2, "ln3": 1.0}[name]
                    nc.vector.tensor_scalar(ve[name][:, :], mv[name][:, :, 1], EPS * scale, None,
                                            ALU.add).then_inc(sem["ve"], 1)

                def gate(m):
                    n = job_f(t, m, 0)
                    dve.wait_ge(sem["tanh"], val("tanh", t, m + 1))
                    nc.vector.scalar_tensor_tensor(tb[:, m % 2, :], tb[:, m % 2, :], 1.0, dense[bank(t, n)][:, :],
                                                   ALU.add, ALU.mult).then_inc(sem["freev"], 1)

                def up(m):
                    n = job_f(t, m, 1)
                    dve.wait_ge(sem["dense"], val("dense", t, n + 1))
                    taken(dve, t, job_f(t, m, 0))
                    nc.vector.scalar_tensor_tensor(tb[:, m % 2, :], tb[:, m % 2, :], S_H / (2 * (S_X * S_W4) ** 2),
                                                   dense[bank(t, n)][:, :], ALU.mult, ALU.mult).then_inc(sem["freev"], 1)

                def o_norm(g):
                    dve.wait_ge(sem["sumc"], val("sumc", t, g + 1))
                    link(t, nc.vector.reciprocal(rec[:, :], rec[:, :]))
                    dve.wait_ge(sem["oc"], val("oc", t, g + 1))
                    linked(t)
                    nc.vector.tensor_tensor(rec[:, :], rec[:, :], osb[:, :], ALU.mult).then_inc(sem["on"], 1)

                def y_moments(i):
                    taken(dve, t, j["D"] + i)
                    moments(t, "lo", lambda i: stage[:, i % 2, :], [i])
                    mean, var, q = mv["lo"][:, i, 0:1], mv["lo"][:, i, 1:2], ve["lo"][:, i:i + 1]
                    link(t, nc.vector.tensor_tensor(q, mean, mean, ALU.mult))
                    linked(t)
                    link(t, nc.vector.tensor_scalar(q, q, EPS, EPS * RMS_EPS * (S_H * S_W4) ** 2, ALU.mult, ALU.add))
                    linked(t)
                    n_ve[0] += 1
                    nc.vector.scalar_tensor_tensor(q, var, 1.0 + EPS, q, ALU.mult, ALU.add).then_inc(sem["ve"], 1)

                def y_norm(i):
                    dve.wait_ge(sem["rs"], val("rs", t, n_y[0] + i + 1))
                    normalise("lo", stage[:, i % 2, :], stage[:, i % 2, :], i).then_inc(sem["yn"], 1)

                if att:
                    for c in range(KC):
                        low("P1", c, xt[:, 1, c, :], S_X, xt[:, 0, c, :])
                if ffn:
                    moments(t, "ln2", lambda i: z[:, i, :], range(NT), lambda i: taken(dve, t, j["WO"] + i))
                    ask_rstd("ln2")
                if att:
                    low("C", 0, ct[:, 1, :], S_C / (S_X * S_W), ct[:, 0, :])
                if ffn:
                    dve.wait_ge(sem["rs"], val("rs", t, 1))
                    for i in range(NT):
                        normalise("ln2", z[:, i, :], z[:, i, :], i).then_inc(sem["z2"], 1)
                if att:
                    low("Q", 0, qk[:, 1, 0, :], HD ** -0.5 * S_QK / (S_X * S_WQ), qk[:, 0, 0, :])
                    for g in range(NG):
                        low("K", g, qk[:, 3, g, :], S_QK / (S_C * S_W), qk[:, 2, g, :])
                    low("Q1", 0, qk[:, 1, 1, :], HD ** -0.5 * S_QK / (S_X * S_WQ), qk[:, 0, 1, :])
                if ffn:
                    moments(t, "ln3", lambda i: x1[:, i, :], range(NT),
                            lambda i: dve.wait_ge(sem["add2"], val("add2", t, i + 1)))
                    ask_rstd("ln3")
                if att:
                    for g in range(2, NG):
                        low("Q1", g - 1, qk[:, 1, g, :], HD ** -0.5 * S_QK / (S_X * S_WQ), qk[:, 0, g, :])
                if ffn:
                    dve.wait_ge(sem["rs"], val("rs", t, 2))
                    for i in range(NT):
                        normalise("ln3", xn2[:, i, :], x1[:, i, :], i).then_inc(sem["ln3"], 1)
                    n_ve[0] = 2
                    for c in range(KC):
                        low("X2", c, x2t[:, 1, c, :], S_X, x2t[:, 0, c, :])
                n_y = [3 if nxt else 2]
                if not att:
                    for m in range(MI):
                        gate(m)
                        up(m)
                    for i in range(NT):
                        y_moments(i)
                        y_norm(i)
                    return
                if isinstance(t, int) and t == 0:
                    dve.wait_ge(s_mask, 2)
                for k in range(H * NT):
                    i, slot = k % NT, k // 2
                    dve.wait_ge(sem["mx"], val("mx", t, k + 1))
                    apart()
                    wide = P * (i + 1)
                    nc.vector.tensor_tensor_reduce(out=score[k % 2][:, 0:wide], in0=score[k % 2][:, 0:wide],
                                                   in1=mmax[:, L - wide:L], scale=1.0, scalar=-3e38,
                                                   op0=ALU.add, op1=ALU.max,
                                                   accum_out=mcol[:, k:k + 1]).then_inc(sem["mxfree"], 1)
                    for m in range(F_EARLY if ffn and k % 2 == 1 else 0):
                        if slot == mx_done(2 * m) + 2:
                            gate(m)
                        if slot == mx_done(2 * m + 1) + 2:
                            up(m)
                dve.wait_ge(sem["mxfree"], val("mxfree", t, H * NT))
                nc.vector.tensor_scalar(mh[:, :], mcol[:, :], -1.0 / ROW_MAX, None, ALU.mult).then_inc(sem["mh"], 1)
                if ffn:
                    for m in range(F_EARLY):
                        if mx_done(2 * m) + 2 >= SLOTS:
                            gate(m)
                        if mx_done(2 * m + 1) + 2 >= SLOTS:
                            up(m)
                    gate(F_EARLY)
                    up(F_EARLY)
                for slot in range(SLOTS):
                    if nxt and slot == LN1_SLOT:
                        dve.wait_ge(sem["xin"], val("xin", t, 16))
                        moments(t, "ln1", lambda i: xin[:, i, :], range(NT))
                        ask_rstd("ln1")
                        n_ln1 = n_ve[0]
                    if nxt and LN1_SLOT + 2 <= slot < LN1_SLOT + 2 + NT:
                        i = slot - LN1_SLOT - 2
                        dve.wait_ge(sem["rs"], val("rs", t, n_ln1))
                        normalise("ln1", xin[:, i, :], xin[:, i, :], i).then_inc(sem["ln1"], 1)
                    if ffn:
                        for m in range(F_EARLY + 1, MI):
                            if slot == late_done(m, 0) + 1:
                                gate(m)
                            if slot == late_done(m, 1) + 1:
                                up(m)
                        for i in range(NT):
                            if slot == down_done(i) + 3:
                                y_norm(i)
                            if slot == down_done(i) + 2:
                                y_moments(i)
                    if slot % (2 * NT) == 0 and slot > 0:
                        o_norm(slot // (2 * NT) - 1)
                o_norm(NG - 1)
                if ffn:
                    for i in range(NT):
                        if down_done(i) + 2 >= SLOTS:
                            y_moments(i)
                        if down_done(i) + 3 >= SLOTS:
                            y_norm(i)

            prepare()
            step(0, True, False, True)
            with dve.Fori(1, B - 1) as t:
                step(t, True, True, True)
            step(B - 1, True, True, False)
            step(B, False, True, False)

        @block.gpsimd
        def _(pool):
            def power(t, name, k, i0=0, i1=NT):
                pool.wait_ge(sem["ve"], k if t is None else val("ve", t, k))
                nc.gpsimd.tensor_tensor(rs[name][:, i0:i1], ve[name][:, i0:i1], half[:, 0:i1 - i0],
                                        ALU.pow).then_inc(sem["rs"], 1)

            def step(t, att, ffn, nxt):
                k = 0
                if ffn:
                    power(t, "ln2", 1)
                    pool.wait_ge(sem["xres"], val("xres", t, 0))
                    for i in range(NT):
                        pool.wait_ge(sem["z2"], val("z2", t, i + 1))
                        nc.gpsimd.tensor_tensor(x1[:, i, :], x1[:, i, :], z[:, i, :], ALU.add).then_inc(sem["add2"], 1)
                    power(t, "ln3", 2)
                    k = 2
                n_y = (2 if ffn else 0) + (1 if nxt else 0)

                def h_low(m):
                    pool.wait_ge(sem["hh"], val("hh", t, m + 1))
                    nc.gpsimd.tensor_tensor(ht[:, 1, m, :], tb[:, m % 2, :], ht[:, 0, m, :],
                                            ALU.subtract).then_inc(sem["hl"], 1)

                def o_low(g):
                    pool.wait_ge(sem["oh"], val("oh", t, g + 1))
                    nc.gpsimd.tensor_tensor(ot[:, 1, g, :], rec[:, :], ot[:, 0, g, :],
                                            ALU.subtract).then_inc(sem["ol"], 1)

                def y_add(i):
                    pool.wait_ge(sem["yn"], val("yn", t, i + 1))
                    nc.gpsimd.tensor_tensor(stage[:, i % 2, :], stage[:, i % 2, :], x1[:, i, :],
                                            ALU.add).then_inc(sem["po"], 1)

                if not att:
                    for m in range(MI):
                        h_low(m)
                    for i in range(NT):
                        power(t, "lo", n_y + i + 1, i, i + 1)
                        y_add(i)
                    return
                if ffn:
                    for m in range(F_EARLY + 1):
                        h_low(m)
                for slot in range(SLOTS):
                    if nxt and slot == LN1_SLOT:
                        power(t, "ln1", n_y)
                    if slot % (2 * NT) == 3 and slot > 2 * NT:
                        o_low(slot // (2 * NT) - 1)
                    if ffn:
                        for m in range(F_EARLY + 1, MI):
                            if slot == late_done(m, 1) + 2:
                                h_low(m)
                        for i in range(NT):
                            if slot == down_done(i) + 3:
                                y_add(i)
                            if slot == down_done(i) + 2:
                                power(t, "lo", n_y + i + 1, i, i + 1)
                o_low(NG - 1)
                if ffn:
                    for i in range(NT):
                        if down_done(i) + 2 >= SLOTS:
                            power(t, "lo", n_y + i + 1, i, i + 1)
                        if down_done(i) + 3 >= SLOTS:
                            y_add(i)

            nc.gpsimd.memset(mmax[:, :], 0.0).then_inc(s_mask, 1)
            pool.wait_ge(s_mask, 1)
            nc.gpsimd.affine_select(out=mmax[:, :], in_=mmax[:, :], compare_op=ALU.is_ge, fill=-1e30, base=L - P,
                                    pattern=[[-1, L]], channel_multiplier=1).then_inc(s_mask, 1)
            pool.wait_ge(s_half, 1)
            power(None, "ln1", 1)
            step(0, True, False, True)
            with pool.Fori(1, B - 1) as t:
                step(t, True, True, True)
            step(B - 1, True, True, False)
            step(B, False, True, False)

        @block.sync
        def _(sp):
            rows = lambda a: a.rearrange("(i p) d -> p i d", p=P)

            def step(t, att, ffn, nxt):
                j = jobs(t)
                if nxt:
                    sp.wait_ge(sem["spare"], val("spare", t, 4))
                    sp.dma_start(xin[:, :, :], rows(x[t + 1, :, :])).then_inc(sem["xin"], 16)
                if att:
                    half_g = NG // 2
                    for last, hi, dst, slots, done, lo_g, hi_g in (
                            (j["K"] + NG - 1, 2, kst, (0, 0, 1), "kstk", 0, NG),
                            (job_q(t, half_g - 1), 0, qst, (0, 1, 0), "qstk0", 0, half_g),
                            (job_q(t, NG - 1), 0, qst, (0, 1, 0), "qstk1", half_g, NG)):
                        taken(sp, t, last)
                        for slot, s in enumerate(slots):
                            for a in range(HG):
                                sp.dma_start(
                                    dst[HD * slot:HD * slot + HD, :, :].rearrange("p (g a) l -> p g a l", a=HG)[:, lo_g:hi_g, a, :],
                                    qk[HD * a:HD * a + HD, hi + s, lo_g:hi_g, :]).then_inc(sem[done], 16)
                    taken(sp, t, j["MT"])
                    sp.dma_start(qst[P - 1:P, :, :].rearrange("p h (i q) -> p (h i) q", q=P),
                                 mrow[:, :]).then_inc(sem["mrow"], 16)
                if ffn:
                    for i in range(NT):
                        sp.wait_ge(sem["po"], val("po", t, i + 1))
                        sp.dma_start(out[t - 1, P * i:P * i + P, :], stage[:, i % 2, :]).then_inc(sem[f"out{i % 2}"], 16)
                        if att:
                            sp.dma_start(x1[:, i, :], x[t, P * i:P * i + P, :]).then_inc(sem["xres"], 16)

            sp.sem_inc(sem["out0"], 16)
            sp.sem_inc(sem["out1"], 16)
            sp.dma_start(raw_wqd, wq_down.rearrange("(r p) d -> p r d", p=P)).then_inc(s_w, 16)
            sp.dma_start(raw_wqu, wq_up_t.rearrange("(r p) d -> p r d", p=P)).then_inc(s_w, 16)
            sp.dma_start(qf[:, 6 * D:8 * D].rearrange("p (a b) -> p a b", a=2)[:, 0, :], k_up_t).then_inc(s_w, 16)
            sp.dma_start(qf[:, 6 * D:8 * D].rearrange("p (a b) -> p a b", a=2)[:, 1, :], v_up_t).then_inc(s_w, 16)
            sp.dma_start(raw_wkv, wkv_down_t.rearrange("(r p) d -> p r d", p=P)).then_inc(s_w, 16)
            sp.dma_start(raw_wo, wo_t.rearrange("(r p) d -> p r d", p=P)).then_inc(s_w, 16)
            for k, (dst, src) in enumerate((
                    (packed[:, 0:GUW].rearrange("p (u w) -> p u w", w=D // 8), gu_packed.rearrange("(u p) w -> p u w", p=P)),
                    (packed[:, GUW:W].rearrange("p (u w) -> p u w", w=I // 8), dn_packed.rearrange("(u p) w -> p u w", p=P)),
                    (sc16[:, 0:2 * MI * GROUPS].rearrange("p (u g) -> p u g", g=GROUPS), gu_scales.rearrange("(u p) g -> p u g", p=P)),
                    (sc16[:, 2 * MI * GROUPS:].rearrange("p (u g) -> p u g", g=MI), dn_scales.rearrange("(u p) g -> p u g", p=P)))):
                sp.dma_start(dst, src).then_inc(s_w4, 16)
            for dst, src in ((tri_sb, tri), (id32, eye32), (id16, eye16), (idbig, eye_big)):
                sp.dma_start(dst[:, :], src).then_inc(s_const, 16)
            sp.dma_start(xin[:, :, :], rows(x[0, :, :])).then_inc(sem["xin"], 16)
            for i in range(NT):
                sp.dma_start(x1[:, i, :], x[0, P * i:P * i + P, :]).then_inc(sem["xres"], 16)
            sp.wait_ge(s_prep_lo, KC)
            sp.wait_ge(s_raw_lo, 4)
            sp.dma_start(qst[96:P - 1, :, :], aug_q[0:HD - 1, :, :]).then_inc(s_aug, 16)
            sp.dma_start(kst[96:P, :, :], aug_k).then_inc(s_aug, 16)
            step(0, True, False, True)
            with sp.Fori(1, B - 1) as t:
                step(t, True, True, True)
            step(B - 1, True, True, False)
            step(B, False, True, False)
            sp.wait_ge(sem["out0"], 16 + 32 * B)
            sp.wait_ge(sem["out1"], 16 + 32 * B)


def constants():
    slopes = np.array([(2.0 ** (-2.0 ** (-(np.log2(H) - 3)))) ** i for i in range(1, H + 1)], np.float32)
    aug_q = np.zeros((HD, H, L), np.float16)
    aug_k = np.zeros((HD, H, L), np.float16)
    pos = np.arange(L, dtype=np.float16)
    left = slopes.astype(np.float64) * S_SCORE
    for n in range(3):
        part = left.astype(np.float16)
        left = left - part
        aug_q[2 * n] = part[:, None]
        aug_k[2 * n] = pos[None]
        aug_q[2 * n + 1] = -pos[None]
        aug_k[2 * n + 1] = part[:, None]
    aug_k[HD - 1] = ROW_MAX
    tri = np.where(np.arange(P)[None] < np.arange(P)[:, None], -60000.0, 0.0).astype(np.float16)
    eye = np.eye(P)
    return {"aug_q": aug_q, "aug_k": aug_k, "tri": tri,
            "eye32": eye.astype(np.float32), "eye16": eye.astype(np.float16), "eye_big": (1024 * eye).astype(np.float16)}


def kernel(L0_attn_hidden_states, L0_attn_Wq_down, L0_attn_Wq_up, L0_attn_Wkv_down, L0_attn_k_up, L0_attn_v_up,
           L0_attn_Wo, L0_ffn_gate_up_packed, L0_ffn_gate_up_scales, L0_ffn_down_packed, L0_ffn_down_scales):
    import concourse.bacc as bacc
    from concourse.bass_utils import run_bass_kernel_spmd
    a = np.asarray
    arrays = {
        "x": a(L0_attn_hidden_states),
        "wq_down": a(L0_attn_Wq_down), "wq_up_t": a(L0_attn_Wq_up).T, "wkv_down_t": a(L0_attn_Wkv_down).T,
        "k_up_t": a(L0_attn_k_up).transpose(1, 0, 2).reshape(RKV, D),
        "v_up_t": a(L0_attn_v_up).transpose(1, 0, 2).reshape(RKV, D),
        "wo_t": a(L0_attn_Wo).T,
        "gu_packed": a(L0_ffn_gate_up_packed), "gu_scales": a(L0_ffn_gate_up_scales).T,
        "dn_packed": a(L0_ffn_down_packed), "dn_scales": a(L0_ffn_down_scales).T,
        **constants(),
    }
    arrays = {n: np.ascontiguousarray(v) for n, v in arrays.items()}
    nc = bacc.Bacc("TRN2", target_bir_lowering=False, num_devices=1)
    aps = {n: nc.dram_tensor(n, v.shape, mybir.dt.from_np(v.dtype), kind="ExternalInput").ap() for n, v in arrays.items()}
    out = nc.dram_tensor("out", (B, L, D), mybir.dt.float32, kind="ExternalOutput").ap()
    nc.disable_value_cache = True
    layer_program(nc, *aps.values(), out)
    r = run_bass_kernel_spmd(nc, [arrays], core_ids=[0])
    return r.results[0]["out"]
```
